# Optimizing a Trainium2 kernel written in Bass

```python
import numpy as np
import jax
import jax.numpy as jnp

def _softmax(x, axis=-1):
    return jax.nn.softmax(x, axis=axis)

def _gelu(x):
    return jax.nn.gelu(x, approximate=True)

def _silu(x):
    return jax.nn.silu(x)

def _sigmoid(x):
    return jax.nn.sigmoid(x)

def _layernorm(x, axis=-1, eps=1e-05):
    m = jnp.mean(x, axis=axis, keepdims=True)
    v = jnp.var(x, axis=axis, keepdims=True)
    return (x - m) / jnp.sqrt(v + eps)

def _scatter_add(tgt, idx, src, axis=0):
    return tgt.at[idx].add(src)

def _segment_sum(src, seg, n):
    return jax.ops.segment_sum(src, seg, n)
kernel_name = 'mk_perceiver_d1_seqx_r4_7192e1'

def setup_inputs(seed: int=0):
    np.random.seed(seed)
    _w = jnp.asarray

    def _rec_inputs():
        import jax
        import jax.numpy as jnp
        _rk = jax.random.key(seed)
        x = -0.000125 + 0.9999 * jax.random.normal(jax.random.fold_in(_rk, 1), (8, 64, 256), jnp.float32)
        _lenS = 64 - jax.random.randint(jax.random.fold_in(_rk, 7), (8,), 0, max(1, 64 // 4) + 1, jnp.int32)
        _lenS2 = 1601 - jax.random.randint(jax.random.fold_in(_rk, 8), (8,), 0, max(1, 1601 // 4) + 1, jnp.int32)
        _ctx_1024P = jax.random.normal(jax.random.fold_in(_rk, 11), (8, 16, 256), jnp.float32)
        _ctx_1024c = jax.random.dirichlet(jax.random.fold_in(_rk, 511), 0.3 * jnp.ones((16,), jnp.float32), (8, 1601))
        _ctx_1024t = jnp.einsum('bsk,bkd->bsd', _ctx_1024c, _ctx_1024P)
        _ctx_1024t = _ctx_1024t * jax.lax.rsqrt(jnp.mean(jnp.square(_ctx_1024t)) + 1e-12) * 0.953939
        ctx_1024 = -1.52775e-05 + 0.999936 * (_ctx_1024t + 0.3 * jax.random.normal(jax.random.fold_in(_rk, 611), (8, 1601, 256), jnp.float32))
        return (x, ctx_1024)
    x, ctx_1024 = _rec_inputs()

    def _L0_xattn_setup():
        import jax, jax.numpy as jnp
        import numpy as np
        D_MODEL = 256
        key = jax.random.key(seed)
        ks = jax.random.split(key, 11)
        B, Sq, Skv, D = (16, 512, 512, D_MODEL)
        s = 1.0 / np.sqrt(D)
        return {'q': jax.random.normal(ks[0], (B, Sq, D), jnp.float32), 'k': jax.random.normal(ks[1], (B, Skv, D), jnp.float32), 'v': jax.random.normal(ks[2], (B, Skv, D), jnp.float32), 'Wq': jax.random.normal(ks[3], (D, D), jnp.float32) * s, 'bq': jnp.zeros((D,), jnp.float32), 'Wk': jax.random.normal(ks[4], (D, D), jnp.float32) * s, 'bk': jnp.zeros((D,), jnp.float32), 'Wv': jax.random.normal(ks[5], (D, D), jnp.float32) * s, 'bv': jnp.zeros((D,), jnp.float32), 'Wo': jax.random.normal(ks[6], (D, D), jnp.float32) * s, 'bo': jnp.zeros((D,), jnp.float32)}
    _L0_xattn_all = _L0_xattn_setup()
    _L0_xattn_in = {k: v for k, v in _L0_xattn_all.items() if k in ('Wq', 'bq', 'Wk', 'bk', 'Wv', 'bv', 'Wo', 'bo')}
    del _L0_xattn_all

    def _L0_attn_setup():
        import jax, jax.numpy as jnp
        import numpy as np
        import math
        B, S, D_IN, D_KQ, D_OUT = (4, 512, 256, 256, 256)
        key = jax.random.key(seed)
        ks = jax.random.split(key, 7)
        sc = 0.02
        return {'x': jax.random.normal(ks[0], (B, S, D_IN), jnp.float32), 'Wq': jax.random.normal(ks[1], (D_KQ, D_IN), jnp.float32) * sc, 'bq': jax.random.normal(ks[2], (D_KQ,), jnp.float32) * sc, 'Wk': jax.random.normal(ks[3], (D_KQ, D_IN), jnp.float32) * sc, 'bk': jax.random.normal(ks[4], (D_KQ,), jnp.float32) * sc, 'Wv': jax.random.normal(ks[5], (D_OUT, D_IN), jnp.float32) * sc, 'bv': jax.random.normal(ks[6], (D_OUT,), jnp.float32) * sc}
    _L0_attn_all = _L0_attn_setup()
    _L0_attn_in = {k: v for k, v in _L0_attn_all.items() if k in ('Wq', 'bq', 'Wk', 'bk', 'Wv', 'bv')}
    del _L0_attn_all

    def _L0_ffn_setup():
        import jax, jax.numpy as jnp
        import numpy as np
        D = 256
        F = 4 * D
        E = 8
        NS = 2
        TOP_K = 2
        B, S = (2, 256)
        key = jax.random.key(seed)
        ks = jax.random.split(key, 7)
        w = 1.0 / np.sqrt(D)
        wf = 1.0 / np.sqrt(F)
        return {'x': jax.random.normal(ks[0], (B, S, D), jnp.float32), 'centroids': jax.random.normal(ks[1], (E, D), jnp.float32) * w, 'routing_bias': jnp.zeros((E,), jnp.float32), 'Wfc_r': jax.random.normal(ks[2], (E, F, D), jnp.float32) * w, 'Wproj_r': jax.random.normal(ks[3], (E, D, F), jnp.float32) * wf, 'Wfc_sh': jax.random.normal(ks[4], (NS, F, D), jnp.float32) * w, 'Wproj_sh': jax.random.normal(ks[5], (NS, D, F), jnp.float32) * wf}
    _L0_ffn_all = _L0_ffn_setup()
    _L0_ffn_in = {k: v for k, v in _L0_ffn_all.items() if k in ('centroids', 'routing_bias', 'Wfc_r', 'Wproj_r', 'Wfc_sh', 'Wproj_sh')}
    del _L0_ffn_all
    return {'x': x, 'ctx_1024': ctx_1024, 'L0_xattn_Wq': _L0_xattn_in['Wq'], 'L0_xattn_bq': _L0_xattn_in['bq'], 'L0_xattn_Wk': _L0_xattn_in['Wk'], 'L0_xattn_bk': _L0_xattn_in['bk'], 'L0_xattn_Wv': _L0_xattn_in['Wv'], 'L0_xattn_bv': _L0_xattn_in['bv'], 'L0_xattn_Wo': _L0_xattn_in['Wo'], 'L0_xattn_bo': _L0_xattn_in['bo'], 'L0_attn_Wq': _L0_attn_in['Wq'], 'L0_attn_bq': _L0_attn_in['bq'], 'L0_attn_Wk': _L0_attn_in['Wk'], 'L0_attn_bk': _L0_attn_in['bk'], 'L0_attn_Wv': _L0_attn_in['Wv'], 'L0_attn_bv': _L0_attn_in['bv'], 'L0_ffn_centroids': _L0_ffn_in['centroids'], 'L0_ffn_routing_bias': _L0_ffn_in['routing_bias'], 'L0_ffn_Wfc_r': _L0_ffn_in['Wfc_r'], 'L0_ffn_Wproj_r': _L0_ffn_in['Wproj_r'], 'L0_ffn_Wfc_sh': _L0_ffn_in['Wfc_sh'], 'L0_ffn_Wproj_sh': _L0_ffn_in['Wproj_sh']}

def reference(x, ctx_1024, L0_xattn_Wq, L0_xattn_bq, L0_xattn_Wk, L0_xattn_bk, L0_xattn_Wv, L0_xattn_bv, L0_xattn_Wo, L0_xattn_bo, L0_attn_Wq, L0_attn_bq, L0_attn_Wk, L0_attn_bk, L0_attn_Wv, L0_attn_bv, L0_ffn_centroids, L0_ffn_routing_bias, L0_ffn_Wfc_r, L0_ffn_Wproj_r, L0_ffn_Wfc_sh, L0_ffn_Wproj_sh):
    import jax
    import jax.numpy as jnp

    def _L0_xattn_ref(q, k, v, Wq, bq, Wk, bk, Wv, bv, Wo, bo):
        import jax, jax.numpy as jnp
        import numpy as np
        D_MODEL = 256
        D = q.shape[-1]
        query = q @ Wq + bq
        key_p = k @ Wk + bk
        value = v @ Wv + bv
        scores = jnp.einsum('bqd,bkd->bqk', query / jnp.sqrt(jnp.float32(D)), key_p)
        attn = jax.nn.softmax(scores, axis=-1)
        out = jnp.einsum('bqk,bkd->bqd', attn, value)
        return out @ Wo + bo

    def _L0_attn_ref(x, Wq, bq, Wk, bk, Wv, bv):
        import jax, jax.numpy as jnp
        import numpy as np
        import math
        B, S, D_IN, D_KQ, D_OUT = (4, 512, 256, 256, 256)
        Q = jnp.einsum('bsd,kd->bsk', x, Wq) + bq
        K = jnp.einsum('bsd,kd->bsk', x, Wk) + bk
        V = jnp.einsum('bsd,od->bso', x, Wv) + bv
        scale = 1.0 / math.sqrt(D_KQ)
        attn = jnp.einsum('bqk,bsk->bqs', Q, K) * scale
        s = attn.shape[-1]
        causal = jnp.tril(jnp.ones((s, s), dtype=bool))
        attn = jnp.where(causal[None, :, :], attn, -jnp.inf)
        attn = jax.nn.softmax(attn, axis=-1)
        Z = jnp.einsum('bqs,bso->bqo', attn, V)
        return Z

    def _L0_ffn_ref(x, centroids, routing_bias, Wfc_r, Wproj_r, Wfc_sh, Wproj_sh):
        import jax, jax.numpy as jnp
        import numpy as np
        D = 256
        F = 4 * D
        E = 8
        NS = 2
        TOP_K = 2
        B, S = (2, 256)
        raw = jnp.einsum('bsd,ed->bse', x, centroids)
        routing_scores = jax.nn.sigmoid(raw)
        balanced = jax.nn.sigmoid(raw + routing_bias)
        _, top_idx = jax.lax.top_k(balanced, TOP_K)
        gathered = jnp.take_along_axis(routing_scores, top_idx, axis=-1)
        top_w = jax.nn.softmax(gathered, axis=-1)
        combine = jnp.sum(jax.nn.one_hot(top_idx, E, dtype=x.dtype) * top_w[..., None], axis=-2)
        h_sh = jax.nn.gelu(jnp.einsum('bsd,nfd->bsnf', x, Wfc_sh), approximate=False)
        shared_out = jnp.einsum('bsnf,ndf->bsd', h_sh, Wproj_sh)
        h_r = jax.nn.gelu(jnp.einsum('bsd,efd->bsef', x, Wfc_r), approximate=False)
        expert_out = jnp.einsum('bsef,edf->bsed', h_r, Wproj_r)
        routed_out = jnp.einsum('bsed,bse->bsd', expert_out, combine)
        return x + shared_out + routed_out
    x = x + _L0_xattn_ref(_layernorm(x, axis=-1), ctx_1024, ctx_1024, L0_xattn_Wq, L0_xattn_bq, L0_xattn_Wk, L0_xattn_bk, L0_xattn_Wv, L0_xattn_bv, L0_xattn_Wo, L0_xattn_bo)
    x = x + _L0_attn_ref(_layernorm(x, axis=-1), L0_attn_Wq, L0_attn_bq, L0_attn_Wk, L0_attn_bk, L0_attn_Wv, L0_attn_bv)
    x = x + _L0_ffn_ref(_layernorm(x, axis=-1), L0_ffn_centroids, L0_ffn_routing_bias, L0_ffn_Wfc_r, L0_ffn_Wproj_r, L0_ffn_Wfc_sh, L0_ffn_Wproj_sh)
    return x

_drawn_inputs = setup_inputs


def setup_inputs(seed=0):
    import zlib

    import numpy as np

    out = dict(_drawn_inputs(seed))
    spreads = {'L0_xattn_bq': (0.0, 0.1),
     'L0_xattn_bk': (0.0, 2.0),
     'L0_xattn_bv': (0.0, 0.1),
     'L0_xattn_bo': (0.0, 0.1),
     'L0_ffn_routing_bias': (0.0, 0.1)}
    factors = {'L0_attn_Wq': 4.588, 'L0_attn_bq': 21.651, 'L0_attn_Wk': 4.051, 'L0_attn_bk': 64.0}
    for name, (base, spread) in spreads.items():
        noise = np.random.default_rng([zlib.crc32(name.encode()), seed]).standard_normal(out[name].shape)
        drawn = base * np.exp(spread * noise) if base else spread * noise
        out[name] = jnp.asarray(drawn.astype(out[name].dtype))
    for name, factor in factors.items():
        out[name] = (out[name] * factor).astype(out[name].dtype)
    return out
```

```python
from contextlib import ExitStack

import concourse.bass as bass
from concourse import mybir

ALU = mybir.AluOpType
ACT = mybir.ActivationFunctionType
AX_X = mybir.AxisListType.X
F32 = mybir.dt.float32
F32R = mybir.dt.float32r
U32 = mybir.dt.uint32

P = 128
D = 256
C = D // P
B, SQ, KV = 8, 64, 1601
T = B // 2
N = B * SQ
F = 1024
J = F // P
SHARED, ROUTED, TOP = 2, 8, 2
E = SHARED + ROUTED
KT = -(-KV // P)
KREM = KV - (KT - 1) * P
BANK = 512
SCH = -(-KV // BANK)
TG = -(-KT // 4)
STEP_W = C * P + D
EPS = 1e-5
SCALE = 1.0 / 16.0
MASKED = -3.0e38

XWQT, XWKT, XWVT, XWO, AWQ, AWK, AWVT = range(7)
XBQ, XBK, XBV, ABQ, ABK, CENT = range(6)
NCOLS = CENT + ROUTED


def scols(ch):
    return slice(ch * BANK, min(KV, (ch + 1) * BANK))


def build(nc, x_d, ctx_d, ctxT_d, squares_d, cols_d, rows_d, experts_d, out_d):
    with ExitStack() as whole:
        def sb(name, shape, dt=F32, stack=whole):
            return stack.enter_context(nc.sbuf_tensor(name, shape, dt))

        def sem(name):
            return whole.enter_context(nc.semaphore(name))

        ident = sb("ident", [P, P])
        mask = sb("mask", [P, P])
        neghalf = sb("neghalf", [P, T])
        iota8 = sb("iota8", [P, T, ROUTED])
        sel = sb("sel", [E, E, P], F32R)
        cols = sb("cols", [P, C, NCOLS])
        rows = sb("rows", [P, 2 * D + ROUTED])
        vecs = sb("vecs", [P, 10])
        xs = sb("xs", [P, T, D])
        xn = sb("xn", [P, T, D])
        xT = sb("xT", [P, C, N])
        cq = sb("cq", [P, T])
        stats = sb("stats", [P, T, 6])
        mv = sb("mv", [P, T, 2])
        veps = sb("veps", [P, T])
        rstd = sb("rstd", [P, T])
        cmax = sb("cmax", [P, SCH])
        small = sb("small", [P, 8])
        nb = sb("nb", [P, 1])
        lsum = sb("lsum", [P, 2, SCH])
        linv = sb("linv", [P, 2])
        c2 = sb("c2", [P, 1])
        small2 = sb("small2", [P, 8])
        nb2 = sb("nb2", [P, 1])
        lsum2 = sb("lsum2", [P, 1])
        xh = sb("xh", [P, C, N], F32R)
        xl = sb("xl", [P, C, N], F32R)
        rz = sb("rz", [P, 2, T, ROUTED])
        sg = sb("sg", [P, 2, T, ROUTED])
        top8 = sb("top8", [P, T, 8])
        idx8 = sb("idx8", [P, T, 8], U32)
        idxf = sb("idxf", [P, T, TOP])
        hot = sb("hot", [P, TOP, T, ROUTED])
        gat = sb("gat", [P, TOP, T, ROUTED])
        g2 = sb("g2", [P, TOP, T])
        gm = sb("gm", [P, 2, T])
        comb = sb("comb", [P, T, E])
        combTh = sb("combTh", [E, N], F32R)
        combTl = sb("combTl", [E, N], F32R)
        raw = [sb("raw0", [P, J, STEP_W]), None]

        with ExitStack() as phase1:
            ctx, ctxT = [None, None], [None, None]
            for i in range(2):
                ctx[i] = sb(f"ctx{i}", [P, 2, KT, D], F32, phase1)
                ctxT[i] = sb(f"ctxT{i}", [P, 2, C, KV], F32, phase1)
            squares = sb("squares", [P, 7, C, D], F32, phase1)
            aq = sb("aq", [P, C, D], F32, phase1)
            wvo = sb("wvo", [P, C, D], F32, phase1)
            a2 = sb("a2", [P, C, D], F32, phase1)
            bcast = sb("bcast", [P, 3, C, P], F32, phase1)
            qT = sb("qT", [P, C, N], F32, phase1)
            prob = sb("prob", [P, KV], F32, phase1)
            probT = sb("probT", [P, KT, P], F32, phase1)
            mix = sb("mix", [P, D], F32, phase1)
            mixT = sb("mixT", [P, C, P], F32, phase1)
            xn2T = sb("xn2T", [P, C, P], F32, phase1)
            tq = sb("tq", [P, C, P], F32, phase1)
            v2 = sb("v2", [P, D], F32, phase1)
            prob2 = sb("prob2", [P, P], F32, phase1)
            prob2T = sb("prob2T", [P, P], F32, phase1)
            sm = sb("sm", [P, P], F32, phase1)
            sel_f = sb("sel_f", [E, E, P], F32, phase1)
            ones = sb("ones", [P, P], F32, phase1)
        whi, wlo = [None, None], [None, None]
        whi[0] = sb("whi0", [P, J, STEP_W], F32R)
        wlo[0] = sb("wlo0", [P, J, STEP_W], F32R)
        raw[1] = sb("raw1", [P, J, STEP_W])
        whi[1] = sb("whi1", [P, J, STEP_W], F32R)
        wlo[1] = sb("wlo1", [P, J, STEP_W], F32R)
        bc = sb("bc", [P, E, N])
        hraw = sb("hraw", [P, 2, N])
        hhi = sb("hhi", [P, 2, N], F32R)
        hlo = sb("hlo", [P, 2, N], F32R)
        acc = sb("acc", [P, C, N])
        tmp = sb("tmp", [P, C, N])

        psum = whole.enter_context(nc.psum_tensor("psum", [P, 8 * BANK], F32))

        def bank(b, lo=0, n=BANK):
            return psum[:, b * BANK + lo:b * BANK + lo + n]

        SC = 0
        PT = 4
        PO = 6
        MISC = 7

        x_in, query_squares_in, squares_in, cols_in, rows_in = (
            sem("x_in"), sem("query_squares_in"), sem("squares_in"), sem("cols_in"), sem("rows_in"))
        ctx_in = [sem("ctx0_in"), sem("ctx1_in")]
        ctxT_in = [sem("ctxT0_in"), sem("ctxT1_in")]
        raw_in = [sem("raw0_in"), sem("raw1_in")]
        consts = sem("consts")
        pool_own, dve_own, act_own = sem("pool_own"), sem("dve_own"), sem("act_own")
        bcast_ready = sem("bcast_ready")
        fold_ps, fold_act, fold_dve = sem("fold_ps"), sem("fold_act"), sem("fold_dve")
        var_ready, rstd_ready = sem("var_ready"), sem("rstd_ready")
        xn1_ready, xT_ps, xT_sb, q_ps, q_sb, cq_ps, cq_sb = (
            sem("xn1_ready"), sem("xT_ps"), sem("xT_sb"), sem("q_ps"), sem("q_sb"), sem("cq_ps"), sem("cq_sb"))
        scores_ps, nb_ready, exp_done = sem("scores_ps"), sem("nb_ready"), sem("exp_done")
        probT_ps, probT_act, probT_dve = sem("probT_ps"), sem("probT_act"), sem("probT_dve")
        pv_ps, mix_ready, mixT_ps, mixT_sb = sem("pv_ps"), sem("mix_ready"), sem("mixT_ps"), sem("mixT_sb")
        proj_ps, x1_ready, xn2_ready, xn2T_ps, xn2T_sb = (
            sem("proj_ps"), sem("x1_ready"), sem("xn2_ready"), sem("xn2T_ps"), sem("xn2T_sb"))
        tq_ps, tq_sb, c2_sb = sem("tq_ps"), sem("tq_sb"), sem("c2_sb")
        sc2_ps, sm_ready, nb2_ready, prob2_ready = (
            sem("sc2_ps"), sem("sm_ready"), sem("nb2_ready"), sem("prob2_ready"))
        v_ps, v_sb, prob2T_ps, prob2T_sb = sem("v_ps"), sem("v_sb"), sem("prob2T_ps"), sem("prob2T_sb")
        z_ps, x2_ready, xn3_ready, xn3T_ps, xn3T_sb = (
            sem("z_ps"), sem("x2_ready"), sem("xn3_ready"), sem("xn3T_ps"), sem("xn3T_sb"))
        xh_ready, xl_ready = sem("xh_ready"), sem("xl_ready")
        route_ps, rz_ready, sig_ready, gap_ready, gate_exp = (
            sem("route_ps"), sem("rz_ready"), sem("sig_ready"), sem("gap_ready"), sem("gate_exp"))
        comb_ready, combT_ps, combTh_ready, combTl_ready = (
            sem("comb_ready"), sem("combT_ps"), sem("combTh_ready"), sem("combTl_ready"))
        bc_ps, bc_sb = sem("bc_ps"), sem("bc_sb")
        whi_ready, wlo_ready = sem("whi_ready"), sem("wlo_ready")
        hidden_ps, gelu_done, hhi_ready, hlo_ready = (
            sem("hidden_ps"), sem("gelu_done"), sem("hhi_ready"), sem("hlo_ready"))
        down_ps, out_read = sem("down_ps"), sem("out_read")
        acc_add, accT_ps, y_ready, y_out = sem("acc_add"), sem("accT_ps"), sem("y_ready"), sem("y_out")

        PAIR = 2 * J
        TURNS = E // 2
        LEAD = 2
        WLEAD = J + LEAD
        H_BANK, OUT_BANK, BC_BANK = 0, 2, 6

        block = whole.enter_context(nc.Block())

        @block.sync
        def _(sp):
            sp.dma_start(xs[:, :, :], x_d.rearrange("(t p) d -> p t d", p=P)).then_inc(x_in, 16)
            sp.dma_start(squares[:, 0:2], squares_d[:, 0:2]).then_inc(query_squares_in, 16)
            sp.dma_start(cols[:, :, :], cols_d.rearrange("(c p) n -> p c n", p=P)).then_inc(cols_in, 16)
            for t in range(T):
                if t >= 2:
                    sp.wait_ge(scores_ps, SCH * (t - 1))
                sp.dma_start(ctxT[t % 2][:, :, :, :],
                             ctxT_d[2 * t:2 * t + 2].rearrange("b (c p) k -> p b c k", p=P)
                             ).then_inc(ctxT_in[t % 2], 16)
                if t == 0:
                    sp.dma_start(squares[:, 2:7], squares_d[:, 2:7]).then_inc(squares_in, 16)
                    sp.dma_start(rows[:, :], rows_d.partition_broadcast(P)).then_inc(rows_in, 16)
                if t >= 2:
                    sp.wait_ge(pv_ps, t - 1)
                for b in range(2):
                    sp.dma_start(ctx[t % 2][:, b, 0:KT - 1, :],
                                 ctx_d[2 * t + b, 0:(KT - 1) * P].rearrange("(k p) d -> p k d", p=P)
                                 ).then_inc(ctx_in[t % 2], 16)
                    sp.dma_start(ctx[t % 2][0:KREM, b, KT - 1, :],
                                 ctx_d[2 * t + b, (KT - 1) * P:KV]).then_inc(ctx_in[t % 2], 16)
            sp.dma_start(raw[0][:, :, :], experts_d[0]).then_inc(raw_in[0], 16)
            sp.wait_ge(pv_ps, T - 1)
            sp.wait_ge(scores_ps, SCH * (T - 1))
            sp.dma_start(raw[1][:, :, :], experts_d[1]).then_inc(raw_in[1], 16)
            with sp.Fori(1, TURNS) as i:
                sp.wait_ge(wlo_ready, i * PAIR - J)
                sp.dma_start(raw[0][:, :, :], experts_d[bass.ds(2 * i, 1)].rearrange("e p j w -> p (e j) w")
                             ).then_inc(raw_in[0], 16)
                sp.wait_ge(wlo_ready, i * PAIR)
                sp.dma_start(raw[1][:, :, :], experts_d[bass.ds(2 * i + 1, 1)].rearrange("e p j w -> p (e j) w")
                             ).then_inc(raw_in[1], 16)
            sp.wait_ge(y_ready, 2)
            sp.dma_start(out_d.rearrange("(t p) d -> p t d", p=P), xs[:, :, :]).then_inc(y_out, 16)
            sp.wait_ge(y_out, 16)

        @block.gpsimd
        def _(pool):
            own = [0]

            def link(ins):
                own[0] += 1
                ins.then_inc(pool_own, 1)
                pool.wait_ge(pool_own, own[0])

            pool.memset(neghalf[:, :], -0.5).then_inc(consts, 1)
            link(pool.memset(ident[:, :], 0.0))
            pool.affine_select(out=ident[:, :], in_=ident[:, :], compare_op=ALU.not_equal, fill=1.0, base=0,
                               pattern=[[-1, P]], channel_multiplier=1).then_inc(consts, 1)
            pool.memset(ones[:, :], 1.0).then_inc(consts, 1)
            link(pool.memset(mask[:, :], 0.0))
            link(pool.affine_select(out=mask[:, :], in_=mask[:, :], compare_op=ALU.is_ge, fill=MASKED, base=0,
                                    pattern=[[-1, P]], channel_multiplier=1))
            pool.memset(mask[SQ:P, 0:SQ], MASKED).then_inc(consts, 1)
            link(pool.memset(sel_f[:, :, :], 0.0))
            link(pool.affine_select(out=sel_f[:, :, :], in_=sel_f[:, :, :], compare_op=ALU.not_equal, fill=1.0,
                                    base=0, pattern=[[-1, E], [0, P]], channel_multiplier=1))
            pool.tensor_copy(sel[:, :, :], sel_f[:, :, :]).then_inc(consts, 1)
            pool.iota(iota8[:, :, :], pattern=[[0, T], [1, ROUTED]], base=0, channel_multiplier=0,
                      allow_small_or_imprecise_dtypes=True).then_inc(consts, 1)
            pool.memset(comb[:, :, 0:SHARED], 1.0).then_inc(consts, 1)
            pool.wait_ge(consts, 7)
            pool.wait_ge(var_ready, 1)
            pool.tensor_tensor(rstd[:, :], veps[:, :], neghalf[:, :], ALU.pow).then_inc(rstd_ready, 1)
            for t in range(T):
                for norm in range(2):
                    pool.wait_ge(var_ready, 2 + 2 * t + norm)
                    pool.tensor_tensor(rstd[:, t:t + 1], veps[:, t:t + 1], neghalf[:, t:t + 1], ALU.pow
                                       ).then_inc(rstd_ready, 1)

        @block.tensor
        def _(pe):
            def mm(out, lhsT, rhs, first, last):
                return pe.matmul(out, lhsT, rhs, start=first, stop=last)

            def fold(b, left, right):
                for m in range(C):
                    for k in range(C):
                        ins = mm(bank(b, m * D, D), squares[:, left, k, m * P:(m + 1) * P],
                                 squares[:, right, k, :], k == 0, k == C - 1)
                ins.then_inc(fold_ps, 1)

            def fold_vec(at, left, col):
                for m in range(C):
                    for k in range(C):
                        ins = mm(bank(3, D + at + m, 1), squares[:, left, k, m * P:(m + 1) * P],
                                 cols[:, k, col:col + 1], k == 0, k == C - 1)
                return ins

            def fold_dot(at, spread, col):
                for k in range(C):
                    ins = mm(bank(3, D + at, 1), bcast[:, spread, k, :], cols[:, k, col:col + 1],
                             k == 0, k == C - 1)
                return ins

            pe.wait_ge(query_squares_in, 16)
            fold(0, XWQT, XWKT)
            pe.wait_ge(cols_in, 16)
            fold_vec(0, XWKT, XBQ)
            fold_vec(2, XWQT, XBK)
            pe.wait_ge(bcast_ready, 3)
            fold_dot(4, 0, XBK).then_inc(fold_ps, 1)
            pe.wait_ge(consts, 7)
            pe.wait_ge(xn1_ready, T)
            for t in range(T):
                for c in range(C):
                    ins = pe.transpose(bank(PT + t // 2, (t % 2) * D + c * P, P),
                                       xn[:, t, c * P:(c + 1) * P], ident[:, :])
                if t % 2 == 1:
                    ins.then_inc(xT_ps, 1)
            pe.wait_ge(fold_act, 1)
            pe.wait_ge(fold_dve, 1)
            for t in range(T):
                pe.wait_ge(xT_sb, t // 2 + 1)
                tok = slice(t * P, (t + 1) * P)
                for m in range(C):
                    for k in range(C):
                        ins = mm(bank(PO + t // 2, (t % 2) * D + m * P, P), aq[:, k, m * P:(m + 1) * P],
                                 xT[:, k, tok], k == 0, k == C - 1)
                if t % 2 == 1:
                    ins.then_inc(q_ps, 1)
            for t in range(T):
                for k in range(C):
                    ins = mm(bank(0, t, 1), xT[:, k, t * P:(t + 1) * P], vecs[:, 2 + k:3 + k],
                             k == 0, k == C - 1)
            ins.then_inc(cq_ps, 1)

            def scores(t, ch):
                if t == 0 and ch == 0:
                    pe.wait_ge(q_sb, 2)
                    pe.wait_ge(cq_sb, 1)
                if ch == 0:
                    pe.wait_ge(ctxT_in[t % 2], 16 * (t // 2 + 1))
                if t >= 1:
                    pe.wait_ge(exp_done, SCH * (t - 1) + ch + 1)
                s = scols(ch)
                for c in range(C):
                    for b in range(2):
                        ins = mm(psum[b * SQ:(b + 1) * SQ, s], qT[:, c, t * P + b * SQ:t * P + (b + 1) * SQ],
                                 ctxT[t % 2][:, b, c, s], c == 0, c == C - 1)
                ins.then_inc(scores_ps, 1)

            def transpose_probs(t, g):
                if g == 0:
                    pe.wait_ge(exp_done, SCH * (t + 1))
                n = TG * t + g
                if g % 2 == 0 and t >= 1 or g >= 2:
                    if g % 2 == 0:
                        pe.wait_ge(probT_act, n // 2)
                    else:
                        pe.wait_ge(probT_dve, n // 2)
                elif t >= 1:
                    pe.wait_ge(probT_dve, n // 2)
                for k in range(4 * g, min(4 * g + 4, KT)):
                    r = P if k < KT - 1 else KREM
                    ins = pe.transpose(bank(PT + g % 2, (k % 4) * P, P)[0:r, :],
                                       prob[:, k * P:k * P + r], ident[:, :])
                ins.then_inc(probT_ps, 1)

            def weigh(t, k0, k1):
                if k0 == 0:
                    pe.wait_ge(ctx_in[t % 2], 64 * (t // 2 + 1))
                    pe.wait_ge(probT_act, 2 * (t + 1))
                    pe.wait_ge(probT_dve, 2 * (t + 1))
                    if t >= 1:
                        pe.wait_ge(mix_ready, t)
                for k in range(k0, k1):
                    r = P if k < KT - 1 else KREM
                    for b in range(2):
                        ins = mm(bank(PO, 0, D)[b * SQ:(b + 1) * SQ, :], probT[0:r, k, b * SQ:(b + 1) * SQ],
                                 ctx[t % 2][0:r, b, k, :], k == 0, k == KT - 1)
                if k1 == KT:
                    ins.then_inc(pv_ps, 1)

            def chain_mixT(t):
                pe.wait_ge(mix_ready, t + 1)
                if t >= 1:
                    pe.wait_ge(xn3T_sb, t)
                for c in range(C):
                    ins = pe.transpose(bank(MISC, c * P, P), mix[:, c * P:(c + 1) * P], ident[:, :])
                ins.then_inc(mixT_ps, 1)

            def chain_proj(t):
                pe.wait_ge(mixT_sb, t + 1)
                if t == 0:
                    pe.wait_ge(fold_act, 2)
                for c in range(C):
                    ins = mm(bank(MISC, 0, D), mixT[:, c, :], wvo[:, c, :], c == 0, c == C - 1)
                ins.then_inc(proj_ps, 1)

            def chain_xn2T(t):
                pe.wait_ge(xn2_ready, t + 1)
                for c in range(C):
                    ins = pe.transpose(bank(MISC, c * P, P), xn[:, t, c * P:(c + 1) * P], ident[:, :])
                ins.then_inc(xn2T_ps, 1)

            def chain_tq(t):
                pe.wait_ge(xn2T_sb, t + 1)
                if t == 0:
                    pe.wait_ge(fold_act, 3)
                    pe.wait_ge(fold_dve, 3)
                for m in range(C):
                    for k in range(C):
                        mm(bank(MISC, m * P, P), a2[:, k, m * P:(m + 1) * P], xn2T[:, k, :],
                           k == 0, k == C - 1)
                for k in range(C):
                    ins = mm(bank(MISC, D, 1), xn2T[:, k, :], vecs[:, 7 + k:8 + k], k == 0, k == C - 1)
                ins.then_inc(tq_ps, 1)

            def chain_scores(t):
                pe.wait_ge(tq_sb, C * (t + 1))
                pe.wait_ge(c2_sb, t + 1)
                for c in range(C):
                    ins = mm(bank(MISC, 0, P), tq[:, c, :], xn2T[:, c, :], c == 0, c == C - 1)
                ins.then_inc(sc2_ps, 1)

            def chain_v(t):
                pe.wait_ge(sm_ready, t + 1)
                for c in range(C):
                    ins = mm(bank(MISC, 0, D), xn2T[:, c, :], squares[:, AWVT, c, :], c == 0, c == C - 1)
                ins.then_inc(v_ps, 1)

            def chain_prob2T(t):
                pe.wait_ge(prob2_ready, t + 1)
                pe.wait_ge(v_sb, t + 1)
                pe.transpose(bank(MISC, 0, P), prob2[:, :], ident[:, :]).then_inc(prob2T_ps, 1)

            def chain_z(t):
                pe.wait_ge(prob2T_sb, t + 1)
                mm(bank(MISC, 0, D), prob2T[:, :], v2[:, :], True, True).then_inc(z_ps, 1)

            def chain_xn3T(t):
                pe.wait_ge(xn3_ready, t + 1)
                for c in range(C):
                    ins = pe.transpose(bank(MISC, c * P, P), xn[:, t, c * P:(c + 1) * P], ident[:, :])
                ins.then_inc(xn3T_ps, 1)

            scores(0, 0)
            pe.wait_ge(squares_in, 16)
            pe.wait_ge(bcast_ready, 3)
            scores(0, 1)
            scores(0, 2)
            for m in range(C):
                for k in range(C):
                    ins = mm(bank(PT, m * D, D), squares[:, XWVT, k, m * P:(m + 1) * P],
                             squares[:, XWO, k, :], k == 0, k == C - 1)
            ins.then_inc(fold_ps, 1)
            for m in range(C):
                for k in range(C):
                    ins = mm(bank(PT + 1, m * D, D), squares[:, AWQ, k, m * P:(m + 1) * P],
                             squares[:, AWK, k, :], k == 0, k == C - 1)
            ins.then_inc(fold_ps, 1)
            for k in range(C):
                mm(bank(PO, 0, D), bcast[:, 1, k, :], squares[:, XWO, k, :], k == 0, k == C - 1)
            for m in range(C):
                for k in range(C):
                    mm(bank(PO, D + m, 1), squares[:, AWK, k, m * P:(m + 1) * P],
                       cols[:, k, ABQ:ABQ + 1], k == 0, k == C - 1)
                for k in range(C):
                    mm(bank(PO, D + 2 + m, 1), squares[:, AWQ, k, m * P:(m + 1) * P],
                       cols[:, k, ABK:ABK + 1], k == 0, k == C - 1)
            for k in range(C):
                ins = mm(bank(PO, D + 4, 1), bcast[:, 2, k, :], cols[:, k, ABK:ABK + 1], k == 0, k == C - 1)
            ins.then_inc(fold_ps, 1)
            scores(0, 3)
            pe.wait_ge(fold_act, 3)
            pe.wait_ge(fold_dve, 3)
            for t in range(T):
                chain = t - 1
                nxt = t + 1
                transpose_probs(t, 0)
                if chain >= 0:
                    chain_mixT(chain)
                transpose_probs(t, 1)
                if chain >= 0:
                    chain_proj(chain)
                transpose_probs(t, 2)
                transpose_probs(t, 3)
                if nxt < T:
                    scores(nxt, 0)
                if chain >= 0:
                    chain_xn2T(chain)
                if nxt < T:
                    scores(nxt, 1)
                if chain >= 0:
                    chain_tq(chain)
                if nxt < T:
                    scores(nxt, 2)
                if chain >= 0:
                    chain_scores(chain)
                if nxt < T:
                    scores(nxt, 3)
                if chain >= 0:
                    chain_v(chain)
                weigh(t, 0, 5)
                if chain >= 0:
                    chain_prob2T(chain)
                weigh(t, 5, 10)
                if chain >= 0:
                    chain_z(chain)
                weigh(t, 10, KT)
                if chain >= 0:
                    chain_xn3T(chain)
            for step in (chain_mixT, chain_proj, chain_xn2T, chain_tq, chain_scores, chain_v,
                         chain_prob2T, chain_z, chain_xn3T):
                step(T - 1)

            pe.wait_ge(xn3T_sb, T)
            for t in range(T):
                for c in range(C):
                    ins = mm(bank(BC_BANK, t * ROUTED, ROUTED), xT[:, c, t * P:(t + 1) * P],
                             cols[:, c, CENT:CENT + ROUTED], c == 0, c == C - 1)
            ins.then_inc(route_ps, 1)

            def hidden(g, s):
                w, j = (s // J) % 2, s % J
                h = bank(H_BANK + s % 2)
                parts = ((whi, xh), (whi, xl), (wlo, xh))
                for c in range(C):
                    for n, (wp, xp) in enumerate(parts):
                        ins = mm(h, wp[w][:, j, c * P:(c + 1) * P], xp[:, c, :],
                                 c == 0 and n == 0, c == C - 1 and n == len(parts) - 1)
                ins.then_inc(hidden_ps, 1)

            def down(s):
                w, j = (s // J) % 2, s % J
                parts = ((whi, hhi), (wlo, hhi), (whi, hlo))
                for n, (wp, hp) in enumerate(parts):
                    for m in range(C):
                        ins = mm(bank(OUT_BANK + 2 * w + m), wp[w][:, j, C * P + m * P:C * P + (m + 1) * P],
                                 hp[:, s % 2, :], j == 0 and n == 0, j == J - 1 and n == len(parts) - 1)
                ins.then_inc(down_ps, 1)

            pe.wait_ge(xl_ready, T)
            for g in range(LEAD):
                pe.wait_ge(wlo_ready, g + 1)
                hidden(g, g)
            pe.wait_ge(comb_ready, 1)
            for t in range(T):
                ins = pe.transpose(bank(BC_BANK + 1, t * P, P)[0:E, :], comb[:, t, :], ident[:, :])
            ins.then_inc(combT_ps, 1)
            pe.wait_ge(combTl_ready, 1)
            for e in range(E):
                if e >= 2:
                    pe.wait_ge(bc_sb, e - 1)
                mm(bank(BC_BANK + e % 2), sel[:, e, :], combTh[:, :], True, False)
                mm(bank(BC_BANK + e % 2), sel[:, e, :], combTl[:, :], False, True).then_inc(bc_ps, 1)

            def turn(i, last):
                for s in range(PAIR):
                    g = i * PAIR + s
                    pe.wait_ge(hlo_ready, g + 1)
                    if s % J == 0:
                        pe.wait_ge(out_read, 2 * i + s // J + 1)
                    down(s)
                    if not last or s + LEAD < PAIR:
                        pe.wait_ge(gelu_done, g + 1)
                        pe.wait_ge(wlo_ready, g + LEAD + 1)
                        hidden(g + LEAD, s + LEAD)

            with pe.Fori(0, TURNS - 1) as i:
                turn(i, False)
            turn(TURNS - 1, True)
            pe.wait_ge(acc_add, E + 1)
            for t in range(T):
                for c in range(C):
                    ins = pe.transpose(bank(H_BANK + t // 2, (t % 2) * D + c * P, P),
                                       acc[:, c, t * P:(t + 1) * P], ident[:, :])
                if t % 2 == 1:
                    ins.then_inc(accT_ps, 1)

        @block.scalar
        def _(act):
            act.wait_ge(fold_ps, 1)
            act.activation(aq[:, :, :].rearrange("p c d -> p (c d)"), bank(0), ACT.Copy, scale=SCALE
                           ).then_inc(fold_act, 1)
            for h in range(2):
                act.wait_ge(xT_ps, h + 1)
                act.activation(xT[:, :, 2 * h * P:2 * (h + 1) * P].rearrange("p c (t n) -> p t c n", t=2),
                               bank(PT + h).rearrange("p (t c n) -> p t c n", t=2, c=C), ACT.Copy
                               ).then_inc(xT_sb, 1)
            act.wait_ge(fold_dve, 1)
            for h in range(2):
                act.wait_ge(q_ps, h + 1)
                for c in range(C):
                    ins = act.activation(qT[:, c, 2 * h * P:2 * (h + 1) * P].rearrange("p (t n) -> p t n", t=2),
                                         bank(PO + h).rearrange("p (t c n) -> p t c n", t=2, c=C)[:, :, c, :],
                                         ACT.Identity, bias=vecs[:, c:c + 1])
                ins.then_inc(q_sb, 1)
            act.wait_ge(fold_ps, 3)
            act.activation(wvo[:, :, :].rearrange("p c d -> p (c d)"), bank(PT), ACT.Copy).then_inc(fold_act, 1)
            act.wait_ge(fold_ps, 4)
            act.activation(a2[:, :, :].rearrange("p c d -> p (c d)"), bank(PT + 1), ACT.Copy, scale=SCALE
                           ).then_inc(fold_act, 1)

            def exps(t, ch):
                act.wait_ge(nb_ready, t + 1)
                s = scols(ch)
                act.activation(prob[:, s], psum[:, s], ACT.Exp, bias=nb[:, :], accum_out=lsum[:, t % 2, ch:ch + 1]
                               ).then_inc(exp_done, 1)

            def probT_copy(t, g):
                act.wait_ge(probT_ps, TG * t + g + 1)
                act.activation(probT[:, 4 * g:4 * g + 4, :].rearrange("p k n -> p (k n)"), bank(PT + g % 2),
                               ACT.Copy).then_inc(probT_act, 1)

            def xn2T_copy(t):
                act.wait_ge(xn2T_ps, t + 1)
                act.activation(xn2T[:, :, :].rearrange("p c n -> p (c n)"), bank(MISC, 0, D), ACT.Copy
                               ).then_inc(xn2T_sb, 1)

            def tq_copy(t):
                act.wait_ge(tq_ps, t + 1)
                for c in range(C):
                    act.activation(tq[:, c, :], bank(MISC, c * P, P), ACT.Identity, bias=vecs[:, 5 + c:6 + c]
                                   ).then_inc(tq_sb, 1)

            def exp2(t):
                act.wait_ge(nb2_ready, t + 1)
                act.activation(prob2[:, :], sm[:, :], ACT.Exp, bias=nb2[:, :], accum_out=lsum2[:, :]
                               ).then_inc(prob2_ready, 1)

            def prob2T_copy(t):
                act.wait_ge(prob2T_ps, t + 1)
                act.activation(prob2T[:, :], bank(MISC, 0, P), ACT.Copy).then_inc(prob2T_sb, 1)

            def xn3T_copy(t):
                tok = slice(t * P, (t + 1) * P)
                act.wait_ge(xn3T_ps, t + 1)
                act.activation(xT[:, :, tok], bank(MISC, 0, D).rearrange("p (c n) -> p c n", c=C), ACT.Copy
                               ).then_inc(xn3T_sb, 1)
                act.wait_ge(xn3T_sb, t + 1)
                act.activation(xh[:, :, tok], xT[:, :, tok], ACT.Copy).then_inc(xh_ready, 1)

            def split_high(g, s):
                w, j = (s // J) % 2, s % J
                act.activation(whi[w][:, j, :], raw[w][:, j, :], ACT.Copy).then_inc(whi_ready, 1)

            for ch in range(SCH):
                exps(0, ch)
            for t in range(T):
                chain, nxt = t - 1, t + 1
                for g in (0, 2):
                    probT_copy(t, g)
                if t == T - 1:
                    act.wait_ge(raw_in[0], 16)
                    for g in range(J):
                        split_high(g, g)
                if chain >= 0:
                    xn2T_copy(chain)
                    tq_copy(chain)
                    exp2(chain)
                for ch in range(SCH):
                    if nxt < T:
                        exps(nxt, ch)
                    if ch == 1 and chain >= 0:
                        prob2T_copy(chain)
                if chain >= 0:
                    xn3T_copy(chain)
            for step in (xn2T_copy, tq_copy, exp2, prob2T_copy, xn3T_copy):
                step(T - 1)

            act.wait_ge(rz_ready, 2)
            act.activation(sg[:, :, :, :].rearrange("p a t e -> p (a t e)"),
                           rz[:, :, :, :].rearrange("p a t e -> p (a t e)"), ACT.Exp, scale=-1.0
                           ).then_inc(sig_ready, 1)
            act.wait_ge(gap_ready, 1)
            act.activation(g2[:, :, :].rearrange("p k t -> p (k t)"), g2[:, :, :].rearrange("p k t -> p (k t)"),
                           ACT.Exp).then_inc(gate_exp, 1)

            def stage(g, s):
                act.wait_ge(hidden_ps, g + 1)
                if not (isinstance(g, int) and g < 2):
                    act.wait_ge(hlo_ready, g - 1)
                act.activation(hraw[:, s % 2, :], bank(H_BANK + s % 2), ACT.Gelu).then_inc(gelu_done, 1)
                act.wait_ge(gelu_done, g + 1)
                if not (isinstance(g, int) and g < 2):
                    act.wait_ge(down_ps, g - 1)
                act.activation(hhi[:, s % 2, :], hraw[:, s % 2, :], ACT.Copy).then_inc(hhi_ready, 1)

            act.wait_ge(raw_in[1], 16)
            for g in range(LEAD):
                stage(g, g)
                split_high(J + g, J + g)
            act.wait_ge(combT_ps, 1)
            act.activation(combTh[:, :], bank(BC_BANK + 1)[0:E, :], ACT.Copy).then_inc(combTh_ready, 1)
            for e in range(0, E, 1):
                act.wait_ge(bc_ps, e + 1)
                act.activation(bc[:, e, :], bank(BC_BANK + e % 2), ACT.Copy).then_inc(bc_sb, 1)

            def turn(i, last):
                for s in range(PAIR):
                    g = i * PAIR + s
                    if not last or s + LEAD < PAIR:
                        stage(g + LEAD, s + LEAD)
                    if not last or s + WLEAD < PAIR:
                        if (s + WLEAD) % J == 0:
                            w = ((s + WLEAD) // J) % 2
                            act.wait_ge(raw_in[w], 16 * (i + 2 - (0 if (s + WLEAD) >= PAIR else 1)))
                        split_high(g + WLEAD, s + WLEAD)

            with act.Fori(0, TURNS - 1) as i:
                turn(i, False)
            turn(TURNS - 1, True)

        @block.vector
        def _(dve):
            own = [0]

            def link(ins):
                own[0] += 1
                ins.then_inc(dve_own, 1)
                dve.wait_ge(dve_own, own[0])

            def norm(t, ready):
                link(dve.bn_stats(stats[:, t, :], xs[:, t, :]))
                link(dve.bn_aggr(mv[:, t, :], stats[:, t, :]))
                dve.tensor_scalar(veps[:, t:t + 1], mv[:, t, 1:2], EPS, None, ALU.add).then_inc(var_ready, 1)
                dve.wait_ge(rstd_ready, ready)
                return dve.tensor_scalar(xn[:, t, :], xs[:, t, :], mv[:, t, 0:1], rstd[:, t:t + 1],
                                         ALU.subtract, ALU.mult)

            dve.wait_ge(x_in, 16)
            for t in range(T):
                ins = dve.bn_stats(stats[:, t, :], xs[:, t, :])
            link(ins)
            for t in range(T):
                ins = dve.bn_aggr(mv[:, t, :], stats[:, t, :])
            link(ins)
            dve.tensor_scalar(veps[:, :], mv[:, :, 1], EPS, None, ALU.add).then_inc(var_ready, 1)
            dve.wait_ge(consts, 7)
            dve.wait_ge(cols_in, 16)
            for n, col in enumerate((XBQ, XBV, ABQ)):
                for c in range(C):
                    ins = dve.tensor_scalar(bcast[:, n, c, :], ones[:, :], cols[:, c, col:col + 1], None, ALU.mult)
                ins.then_inc(bcast_ready, 1)
            dve.wait_ge(rstd_ready, 1)
            for t in range(T):
                dve.tensor_scalar(xn[:, t, :], xs[:, t, :], mv[:, t, 0:1], rstd[:, t:t + 1],
                                  ALU.subtract, ALU.mult).then_inc(xn1_ready, 1)
            dve.wait_ge(fold_ps, 2)
            dve.tensor_scalar(vecs[:, 0:5], bank(3, D, 5), SCALE, None, ALU.mult).then_inc(fold_dve, 1)
            dve.wait_ge(fold_dve, 1)
            dve.wait_ge(cq_ps, 1)
            dve.tensor_scalar(cq[:, :], bank(0, 0, T), vecs[:, 4:5], None, ALU.add).then_inc(cq_sb, 1)

            def max_chunk(t, ch):
                dve.wait_ge(scores_ps, SCH * t + ch + 1)
                ins = dve.tensor_reduce(cmax[:, ch:ch + 1], psum[:, scols(ch)], AX_X, ALU.max)
                if ch == SCH - 1:
                    link(ins)
                    link(dve.tensor_reduce(small[:, 0:1], cmax[:, :], AX_X, ALU.max))
                    link(dve.tensor_tensor(small[:, 1:2], small[:, 0:1], cq[:, t:t + 1], ALU.add))
                    if t >= 1:
                        dve.wait_ge(exp_done, SCH * t)
                    dve.tensor_tensor(nb[:, :], cq[:, t:t + 1], small[:, 1:2], ALU.subtract).then_inc(nb_ready, 1)

            for ch in range(SCH - 1):
                max_chunk(0, ch)
            dve.wait_ge(fold_ps, 5)
            dve.wait_ge(rows_in, 16)
            dve.tensor_tensor(mix[:, :], bank(PO, 0, D), rows[:, 0:D], ALU.add).then_inc(fold_dve, 1)
            dve.tensor_scalar(vecs[:, 5:10], bank(PO, D, 5), SCALE, None, ALU.mult).then_inc(fold_dve, 1)
            dve.wait_ge(fold_dve, 2)
            for t in range(T):
                ins = dve.tensor_tensor(xs[:, t, :], xs[:, t, :], mix[:, :], ALU.add)
            link(ins)
            max_chunk(0, SCH - 1)

            def probT_copy(t, g):
                dve.wait_ge(probT_ps, TG * t + g + 1)
                if g == TG - 1:
                    ins = dve.tensor_copy(probT[0:KREM, KT - 1, :], bank(PT + g % 2, 0, P)[0:KREM, :])
                else:
                    ins = dve.tensor_copy(probT[:, 4 * g:4 * g + 4, :].rearrange("p k n -> p (k n)"),
                                          bank(PT + g % 2))
                ins.then_inc(probT_dve, 1)

            def mix_scale(t):
                dve.wait_ge(exp_done, SCH * (t + 1))
                link(dve.tensor_reduce(small[:, 2:3], lsum[:, t % 2, :], AX_X, ALU.add))
                link(dve.reciprocal(linv[:, 0:1], small[:, 2:3]))
                dve.wait_ge(pv_ps, t + 1)
                dve.tensor_scalar(mix[:, :], bank(PO, 0, D), linv[:, 0:1], None, ALU.mult).then_inc(mix_ready, 1)

            def mixT_copy(t):
                dve.wait_ge(mixT_ps, t + 1)
                dve.tensor_copy(mixT[:, :, :].rearrange("p c n -> p (c n)"), bank(MISC, 0, D)
                                ).then_inc(mixT_sb, 1)

            def x1_add(t):
                dve.wait_ge(proj_ps, t + 1)
                dve.tensor_tensor(xs[:, t, :], bank(MISC, 0, D), xs[:, t, :], ALU.add).then_inc(x1_ready, 1)

            def norm2(t):
                dve.wait_ge(x1_ready, t + 1)
                norm(t, 2 + 2 * t).then_inc(xn2_ready, 1)

            def c2_copy(t):
                dve.wait_ge(tq_ps, t + 1)
                dve.wait_ge(tq_sb, C * (t + 1))
                dve.tensor_scalar(c2[:, :], bank(MISC, D, 1), vecs[:, 9:10], None, ALU.add).then_inc(c2_sb, 1)

            def softmax2(t):
                dve.wait_ge(sc2_ps, t + 1)
                dve.wait_ge(c2_sb, t + 1)
                dve.tensor_tensor(sm[:, :], bank(MISC, 0, P), mask[:, :], ALU.add).then_inc(sm_ready, 1)
                dve.wait_ge(sm_ready, t + 1)
                link(dve.tensor_reduce(small2[:, 0:1], sm[:, :], AX_X, ALU.max))
                link(dve.tensor_tensor(small2[:, 1:2], small2[:, 0:1], c2[:, :], ALU.add))
                dve.tensor_tensor(nb2[:, :], c2[:, :], small2[:, 1:2], ALU.subtract).then_inc(nb2_ready, 1)

            def v_copy(t):
                dve.wait_ge(v_ps, t + 1)
                dve.tensor_tensor(v2[:, :], bank(MISC, 0, D), rows[:, D:2 * D], ALU.add).then_inc(v_sb, 1)

            def x2_add(t):
                dve.wait_ge(prob2_ready, t + 1)
                link(dve.reciprocal(linv[:, 1:2], lsum2[:, :]))
                dve.wait_ge(z_ps, t + 1)
                dve.scalar_tensor_tensor(xs[:, t, :], bank(MISC, 0, D), linv[:, 1:2], xs[:, t, :],
                                         ALU.mult, ALU.add).then_inc(x2_ready, 1)
                dve.wait_ge(x2_ready, t + 1)
                norm(t, 3 + 2 * t).then_inc(xn3_ready, 1)
                dve.wait_ge(xn3_ready, t + 1)
                link(dve.tensor_tensor(xs[:, t, :], xs[:, t, :], xn[:, t, :], ALU.add))

            def split_x(t):
                tok = slice(t * P, (t + 1) * P)
                dve.wait_ge(xh_ready, t + 1)
                dve.tensor_tensor(xl[:, :, tok], xT[:, :, tok], xh[:, :, tok].bitcast(F32), ALU.subtract
                                  ).then_inc(xl_ready, 1)

            def split_low(g, s):
                w, j = (s // J) % 2, s % J
                dve.wait_ge(whi_ready, g + 1)
                dve.tensor_tensor(wlo[w][:, j, :], raw[w][:, j, :], whi[w][:, j, :].bitcast(F32), ALU.subtract
                                  ).then_inc(wlo_ready, 1)

            for t in range(T):
                chain, nxt = t - 1, t + 1
                if chain >= 0:
                    mixT_copy(chain)
                probT_copy(t, 1)
                if chain >= 0:
                    x1_add(chain)
                probT_copy(t, 3)
                if chain >= 0:
                    norm2(chain)
                for ch in range(SCH):
                    if nxt < T:
                        max_chunk(nxt, ch)
                    if ch == 1 and chain >= 0:
                        c2_copy(chain)
                    if ch == 2 and chain >= 0:
                        softmax2(chain)
                if chain >= 0:
                    v_copy(chain)
                    x2_add(chain)
                mix_scale(t)
                if chain >= 0:
                    split_x(chain)
                if t == T - 1:
                    for g in range(J):
                        split_low(g, g)
            for step in (mixT_copy, x1_add, norm2, c2_copy, softmax2, v_copy, x2_add, split_x):
                step(T - 1)

            dve.wait_ge(route_ps, 1)
            dve.wait_ge(consts, 7)
            zflat = bank(BC_BANK, 0, T * ROUTED).rearrange("p (t e) -> p t e", t=T)
            dve.tensor_copy(rz[:, 0, :, :], zflat).then_inc(rz_ready, 1)
            dve.tensor_tensor(rz[:, 1, :, :], zflat,
                              rows[:, 2 * D:2 * D + ROUTED].unsqueeze(1).to_broadcast([P, T, ROUTED]),
                              ALU.add).then_inc(rz_ready, 1)
            dve.wait_ge(sig_ready, 1)
            sgf = sg[:, :, :, :].rearrange("p a t e -> p (a t e)")
            link(dve.tensor_scalar(sgf, sgf, 1.0, None, ALU.add))
            link(dve.reciprocal(sgf, sgf))
            for t in range(T):
                ins = dve.max(top8[:, t, :], sg[:, 1, t, :])
            link(ins)
            for t in range(T):
                ins = dve.max_index(idx8[:, t, :], top8[:, t, :], sg[:, 1, t, :])
            link(ins)
            link(dve.tensor_copy(idxf[:, :, :], idx8[:, :, 0:TOP]))
            for k in range(TOP):
                ins = dve.tensor_tensor(hot[:, k, :, :], iota8[:, :, :],
                                        idxf[:, :, k:k + 1].to_broadcast([P, T, ROUTED]), ALU.is_equal)
            link(ins)
            for k in range(TOP):
                ins = dve.tensor_tensor(gat[:, k, :, :], hot[:, k, :, :], sg[:, 0, :, :], ALU.mult)
            link(ins)
            link(dve.tensor_reduce(g2[:, :, :], gat[:, :, :, :], AX_X, ALU.add))
            link(dve.tensor_tensor(gm[:, 0, :], g2[:, 0, :], g2[:, 1, :], ALU.max))
            for k in range(TOP):
                ins = dve.tensor_tensor(g2[:, k, :], g2[:, k, :], gm[:, 0, :], ALU.subtract)
            ins.then_inc(gap_ready, 1)
            dve.wait_ge(gate_exp, 1)
            link(dve.tensor_tensor(gm[:, 0, :], g2[:, 0, :], g2[:, 1, :], ALU.add))
            link(dve.reciprocal(gm[:, 1, :], gm[:, 0, :]))
            for k in range(TOP):
                ins = dve.tensor_tensor(g2[:, k, :], g2[:, k, :], gm[:, 1, :], ALU.mult)
            link(ins)
            for k in range(TOP):
                ins = dve.tensor_tensor(gat[:, k, :, :], hot[:, k, :, :],
                                        g2[:, k, :].unsqueeze(2).to_broadcast([P, T, ROUTED]), ALU.mult)
            link(ins)
            dve.tensor_tensor(comb[:, :, SHARED:E], gat[:, 0, :, :], gat[:, 1, :, :], ALU.add
                              ).then_inc(comb_ready, 1)

            def stage(g, s):
                dve.wait_ge(hhi_ready, g + 1)
                dve.tensor_tensor(hlo[:, s % 2, :], hraw[:, s % 2, :], hhi[:, s % 2, :].bitcast(F32),
                                  ALU.subtract).then_inc(hlo_ready, 1)

            def gather(e, w):
                dve.wait_ge(down_ps, J * e + J)
                dve.wait_ge(acc_add, e + 1)
                for m in range(C):
                    if isinstance(e, int):
                        weight = bc[:, e, :]
                    else:
                        weight = bc[:, bass.ds(e, 1), :].rearrange("p e n -> p (e n)")
                    ins = dve.tensor_tensor(tmp[:, m, :], bank(OUT_BANK + 2 * w + m), weight, ALU.mult)
                ins.then_inc(out_read, 1)
                dve.wait_ge(out_read, e + 3)
                dve.tensor_tensor(acc[:, :, :], acc[:, :, :], tmp[:, :, :], ALU.add).then_inc(acc_add, 1)

            dve.memset(tmp[:, :, :], 0.0).then_inc(acc_add, 1)
            dve.memset(acc[:, 0, :], 0.0).then_inc(out_read, 1)
            dve.memset(acc[:, 1, :], 0.0).then_inc(out_read, 1)
            dve.wait_ge(combTh_ready, 1)
            dve.tensor_tensor(combTl[:, :], bank(BC_BANK + 1)[0:E, :], combTh[:, :].bitcast(F32), ALU.subtract
                              ).then_inc(combTl_ready, 1)
            for g in range(LEAD):
                stage(g, g)
                split_low(J + g, J + g)
            dve.wait_ge(bc_sb, E)
            dve.wait_ge(out_read, 2)

            def turn(i, last):
                for s in range(PAIR):
                    g = i * PAIR + s
                    if not last or s + LEAD < PAIR:
                        stage(g + LEAD, s + LEAD)
                    if not last or s + WLEAD < PAIR:
                        split_low(g + WLEAD, s + WLEAD)
                    if s % J == J - 1:
                        gather(2 * i + s // J, s // J)

            with dve.Fori(0, TURNS - 1) as i:
                turn(i, False)
            turn(TURNS - 1, True)
            for h in range(2):
                dve.wait_ge(accT_ps, h + 1)
                dve.tensor_tensor(xs[:, 2 * h:2 * h + 2, :].rearrange("p t d -> p (t d)"), bank(H_BANK + h),
                                  xs[:, 2 * h:2 * h + 2, :].rearrange("p t d -> p (t d)"), ALU.add
                                  ).then_inc(y_ready, 1)


def kernel(**inputs):
    import numpy as np
    import concourse.bacc as bacc
    from concourse import mybir as mb
    from concourse.bass_utils import run_bass_kernel_spmd

    a = {k: np.asarray(v) for k, v in inputs.items()}

    def up(w):
        return w.reshape(-1, J, P, C, P).transpose(0, 4, 1, 3, 2).reshape(-1, P, J, C * P)

    def down(w):
        return w.reshape(-1, D, J, P).transpose(0, 3, 2, 1)

    squares = np.stack([a["L0_xattn_Wq"].T, a["L0_xattn_Wk"].T, a["L0_xattn_Wv"].T, a["L0_xattn_Wo"],
                        a["L0_attn_Wq"], a["L0_attn_Wk"], a["L0_attn_Wv"].T])
    arrays = {
        "x_in_dram": a["x"].reshape(N, D),
        "ctx_dram": a["ctx_1024"],
        "ctxT_dram": a["ctx_1024"].transpose(0, 2, 1),
        "squares_dram": squares.reshape(7, C, P, D).transpose(2, 0, 1, 3),
        "cols_dram": np.concatenate([np.stack([a["L0_xattn_bq"], a["L0_xattn_bk"], a["L0_xattn_bv"],
                                               a["L0_attn_bq"], a["L0_attn_bk"]]),
                                     a["L0_ffn_centroids"]]).T,
        "rows_dram": np.concatenate([a["L0_xattn_bo"], a["L0_attn_bv"], a["L0_ffn_routing_bias"]]),
        "experts_dram": np.concatenate([
            np.concatenate([up(a["L0_ffn_Wfc_sh"]), down(a["L0_ffn_Wproj_sh"])], axis=3),
            np.concatenate([up(a["L0_ffn_Wfc_r"]), down(a["L0_ffn_Wproj_r"])], axis=3)]),
    }
    arrays = {k: np.ascontiguousarray(v) for k, v in arrays.items()}
    nc = bacc.Bacc("TRN2", target_bir_lowering=False, num_devices=1)
    args = [nc.dram_tensor(k, v.shape, mb.dt.from_np(v.dtype), kind="ExternalInput").ap() for k, v in arrays.items()]
    out = nc.dram_tensor("out_dram", (N, D), mb.dt.float32, kind="ExternalOutput").ap()
    build(nc, *args, out)
    r = run_bass_kernel_spmd(nc, [arrays], core_ids=[0])
    return r.results[0]["out_dram"].reshape(B, SQ, D)
```

```python
from contextlib import ExitStack

import concourse.bass as bass
from concourse import mybir

ALU = mybir.AluOpType
ACT = mybir.ActivationFunctionType
AX_X = mybir.AxisListType.X
F32 = mybir.dt.float32
F32R = mybir.dt.float32r
U32 = mybir.dt.uint32

P = 128
D = 256
C = D // P
B, SQ, KV = 8, 64, 1601
T = B // 2
N = B * SQ
F = 1024
J = F // P
SHARED, ROUTED, TOP = 2, 8, 2
E = SHARED + ROUTED
KT = -(-KV // P)
KREM = KV - (KT - 1) * P
BANK = 512
SCH = -(-KV // BANK)
TG = -(-KT // 4)
STEP_W = C * P + D
EPS = 1e-5
SCALE = 1.0 / 16.0
MASKED = -3.0e38

OVER = (TOP * N - ROUTED) // P
SLOTS = ROUTED + OVER
RING = 3
HALF = N // 2
UNITS = 2 * SHARED * J

XWQT, XWKT, XWVT, XWO, AWQ, AWK, AWVT = range(7)
XBQ, XBK, XBV, ABQ, ABK, CENT = range(6)
NCOLS = CENT + ROUTED


def scols(ch):
    return slice(ch * BANK, min(KV, (ch + 1) * BANK))


def plan():
    order = []
    for t in range(T - 1):
        c = t - 1
        chain = (lambda *names: [(name, c) for name in names]) if c >= 0 else (lambda *names: [])
        order += [("T", t, 0), *chain("mixT"), ("T", t, 1), *chain("proj"), ("T", t, 2), ("T", t, 3),
                  ("S", t + 1, 0), *chain("xn2T"), ("S", t + 1, 1), *chain("tq"), ("S", t + 1, 2),
                  *chain("sc"), ("S", t + 1, 3), *chain("v"), ("exp", t + 1, 0), ("exp", t + 1, 1),
                  ("W", t, 0, 5), *chain("probT"), ("exp", t + 1, 2), ("exp", t + 1, 3),
                  ("W", t, 5, 10), *chain("z"), ("W", t, 10, KT), *chain("xn3T")]
    t, c = T - 1, T - 2
    order += [("T", t, 0), ("mixT", c), ("T", t, 1), ("proj", c), ("T", t, 2), ("T", t, 3), ("split", 0),
              ("W", t, 0, 3), ("split", 1), ("xn2T", c), ("W", t, 3, 6), ("split", 2), ("split", 3), ("tq", c),
              ("W", t, 6, 9), ("split", 4), ("sc", c), ("W", t, 9, 11), ("split", 5), ("v", c),
              ("W", t, 11, KT), ("split", 6), ("probT", c), ("split", 7), ("lead", 0), ("lead", 1),
              ("z", c), ("mixT", t), ("unit", 0), ("split", 8), ("xn3T", c), ("proj", t), ("unit", 1), ("split", 9),
              ("unit", 2), ("split", 10), ("xn2T", t), ("unit", 3), ("split", 11), ("tq", t), ("unit", 4),
              ("split", 12), ("sc", t), ("unit", 5), ("split", 13), ("v", t), ("unit", 6), ("split", 14),
              ("probT", t), ("unit", 7), ("split", 15), ("z", t), ("unit", 8), ("unit", 9), ("unit", 10),
              ("xn3T", t), ("unit", 11), ("route", ), ("unit", 12), ("top2", ), ("unit", 13), ("hot", ),
              ("unit", 14), ("rank", ), ("unit", 15), ("place", ), ("unit", 16), ("unit", 17), ("gates", ),
              ("shared_out", 0)]
    order += [("unit", n) for n in range(18, UNITS)] + [("shared_out", 1)]
    return order


def build(nc, x_d, ctx_d, ctxT_d, squares_d, cols_d, rows_d, experts_d, out_d, slot_x_d, slot_y_d):
    with ExitStack() as whole:
        def sb(name, shape, dt=F32, stack=whole):
            return stack.enter_context(nc.sbuf_tensor(name, shape, dt))

        def sem(name):
            return whole.enter_context(nc.semaphore(name))

        ident = sb("ident", [P, P])
        mask = sb("mask", [P, P])
        neghalf = sb("neghalf", [P, T])
        tri = sb("tri", [P, P])
        ones = sb("ones", [P, P])
        iota8 = sb("iota8", [P, T, ROUTED])
        iota128 = sb("iota128", [P, ROUTED])
        over_no = sb("over_no", [P, OVER, ROUTED])
        zeros = sb("zeros", [P, D])
        cols = sb("cols", [P, C, NCOLS])
        rows = sb("rows", [P, 2 * D + ROUTED])
        vecs = sb("vecs", [P, 10])
        xs = sb("xs", [P, T, D])
        xn = sb("xn", [P, T, D])
        xT = sb("xT", [P, C, N])
        cq = sb("cq", [P, T])
        stats = sb("stats", [P, T, 6])
        mv = sb("mv", [P, T, 2])
        veps = sb("veps", [P, T])
        rstd = sb("rstd", [P, T])
        cmax = sb("cmax", [P, SCH])
        small = sb("small", [P, 8])
        nb = sb("nb", [P, 1])
        lsum = sb("lsum", [P, 2, SCH])
        linv = sb("linv", [P, 2])
        c2 = sb("c2", [P, 1])
        small2 = sb("small2", [P, 8])
        nb2 = sb("nb2", [P, 1])
        lsum2 = sb("lsum2", [P, 1])
        xh = sb("xh", [P, C, N], F32R)
        xl = sb("xl", [P, C, N], F32R)
        rz = sb("rz", [P, 2, T, ROUTED])
        sg = sb("sg", [P, 2, T, ROUTED])
        top8 = sb("top8", [P, T, 8])
        idx8 = sb("idx8", [P, T, 8], U32)
        idxf = sb("idxf", [P, T, TOP])
        hot = sb("hot", [P, TOP, T, ROUTED])
        gat = sb("gat", [P, TOP, T, ROUTED])
        chosen = sb("chosen", [P, T, ROUTED])
        before = sb("before", [P, T, ROUTED])
        total = sb("total", [P, ROUTED])
        rank = sb("rank", [P, T, ROUTED])
        count = sb("count", [P, ROUTED])
        over = sb("over", [P, 3, ROUTED])
        ones8 = sb("ones8", [P, ROUTED])
        after = sb("after", [P, OVER, ROUTED])
        expert_f = sb("expert_f", [P, SLOTS])
        expert_of = sb("expert_of", [P, SLOTS], U32)
        base = sb("base", [P, 2, ROUTED])
        row = sb("row", [P, T, ROUTED])
        first = sb("first", [P, T, ROUTED])
        rows_of_f = sb("rows_of_f", [P, TOP, T])
        rows_of = sb("rows_of", [P, TOP, T], U32)
        g2 = sb("g2", [P, TOP, T])
        gap = sb("gap", [P, T])
        gate = sb("gate", [P, TOP, T])
        hraw = sb("hraw", [P, 2, HALF])
        hhi = sb("hhi", [P, 2, HALF], F32R)
        hlo = sb("hlo", [P, 2, HALF], F32R)
        raw = [sb("raw0", [P, J, STEP_W]), None, None]

        with ExitStack() as phase1:
            ctx, ctxT = [None, None], [None, None]
            for i in range(2):
                ctx[i] = sb(f"ctx{i}", [P, 2, KT, D], F32, phase1)
                ctxT[i] = sb(f"ctxT{i}", [P, 2, C, KV], F32, phase1)
            squares = sb("squares", [P, 7, C, D], F32, phase1)
            aq = sb("aq", [P, C, D], F32, phase1)
            wvo = sb("wvo", [P, C, D], F32, phase1)
            a2 = sb("a2", [P, C, D], F32, phase1)
            bcast = sb("bcast", [P, 3, C, P], F32, phase1)
            qT = sb("qT", [P, C, N], F32, phase1)
            prob = sb("prob", [P, KV], F32, phase1)
            probT = sb("probT", [P, KT, P], F32, phase1)
            mix = sb("mix", [P, D], F32, phase1)
            mixT = sb("mixT", [P, C, P], F32, phase1)
            xn2T = sb("xn2T", [P, C, P], F32, phase1)
            tq = sb("tq", [P, C, P], F32, phase1)
            v2 = sb("v2", [P, D], F32, phase1)
            prob2 = sb("prob2", [P, P], F32, phase1)
            prob2T = sb("prob2T", [P, P], F32, phase1)
            sm = sb("sm", [P, P], F32, phase1)
        whi, wlo = [None, None], [None, None]
        whi[0] = sb("whi0", [P, J, STEP_W], F32R)
        wlo[0] = sb("wlo0", [P, J, STEP_W], F32R)
        raw[1] = sb("raw1", [P, J, STEP_W])
        whi[1] = sb("whi1", [P, J, STEP_W], F32R)
        wlo[1] = sb("wlo1", [P, J, STEP_W], F32R)
        raw[2] = sb("raw2", [P, J, STEP_W])
        xrow = sb("xrow", [P, RING, D])
        xrowT = sb("xrowT", [P, C, P])
        hT = sb("hT", [P, 2, BANK])
        y_rows = sb("y_rows", [P, SLOTS, D])
        picked = sb("picked", [P, TOP, T, D])

        psum = whole.enter_context(nc.psum_tensor("psum", [P, 8 * BANK], F32))

        def bank(b, lo=0, n=BANK):
            return psum[:, b * BANK + lo:b * BANK + lo + n]

        SC = 0
        PT = 4
        PO = 6
        CHAIN = 7

        def chain_bank(t):
            return CHAIN if t < T - 1 else PT + 1

        x_in, query_squares_in, squares_in, cols_in, rows_in = (
            sem("x_in"), sem("query_squares_in"), sem("squares_in"), sem("cols_in"), sem("rows_in"))
        ctx_in = [sem("ctx0_in"), sem("ctx1_in")]
        ctxT_in = [sem("ctxT0_in"), sem("ctxT1_in")]
        raw_in = [sem("raw0_in"), sem("raw1_in"), sem("raw2_in")]
        xrow_in = [sem("xrow0_in"), sem("xrow1_in"), sem("xrow2_in")]
        consts = sem("consts")
        pool_own, dve_own, act_own = sem("pool_own"), sem("dve_own"), sem("act_own")
        bcast_ready = sem("bcast_ready")
        fold_ps, fold_act, fold_dve = sem("fold_ps"), sem("fold_act"), sem("fold_dve")
        var_ready, rstd_ready = sem("var_ready"), sem("rstd_ready")
        xn1_ready, xT_ps, xT_sb, q_ps, q_sb, cq_ps, cq_sb = (
            sem("xn1_ready"), sem("xT_ps"), sem("xT_sb"), sem("q_ps"), sem("q_sb"), sem("cq_ps"), sem("cq_sb"))
        scores_ps, nb_ready, exp_done = sem("scores_ps"), sem("nb_ready"), sem("exp_done")
        probT_ps, probT_act, probT_dve = sem("probT_ps"), sem("probT_act"), sem("probT_dve")
        pv_ps, mix_ready, mixT_ps, mixT_sb = sem("pv_ps"), sem("mix_ready"), sem("mixT_ps"), sem("mixT_sb")
        proj_ps, x1_ready, xn2_ready, xn2T_ps, xn2T_sb = (
            sem("proj_ps"), sem("x1_ready"), sem("xn2_ready"), sem("xn2T_ps"), sem("xn2T_sb"))
        tq_ps, tq_sb, c2_sb = sem("tq_ps"), sem("tq_sb"), sem("c2_sb")
        sc2_ps, sm_ready, nb2_ready, prob2_ready = (
            sem("sc2_ps"), sem("sm_ready"), sem("nb2_ready"), sem("prob2_ready"))
        v_ps, v_sb, prob2T_ps, prob2T_sb = sem("v_ps"), sem("v_sb"), sem("prob2T_ps"), sem("prob2T_sb")
        z_ps, x2_ready, xn3_ready, xn3T_ps, xn3T_sb = (
            sem("z_ps"), sem("x2_ready"), sem("xn3_ready"), sem("xn3T_ps"), sem("xn3T_sb"))
        xh_ready, xl_ready = sem("xh_ready"), sem("xl_ready")
        route_ps, rz_ready, sig_ready, gap_ready, tanh_done = (
            sem("route_ps"), sem("rz_ready"), sem("sig_ready"), sem("gap_ready"), sem("tanh_done"))
        chosen_ready, rank_ps, expert_ready, rows_of_ready = (
            sem("chosen_ready"), sem("rank_ps"), sem("expert_ready"), sem("rows_of_ready"))
        slots_zeroed, scattered = sem("slots_zeroed"), sem("scattered")
        whi_ready, wlo_ready = sem("whi_ready"), sem("wlo_ready")
        hidden_ps, gelu_done, hhi_ready, hlo_ready = (
            sem("hidden_ps"), sem("gelu_done"), sem("hhi_ready"), sem("hlo_ready"))
        down_ps, shared_read = sem("down_ps"), sem("shared_read")
        xrowT_ps, xrowT_sb, slot_hidden_ps, slot_gelu = (
            sem("xrowT_ps"), sem("xrowT_sb"), sem("slot_hidden_ps"), sem("slot_gelu"))
        slot_down_ps, y_rows_ready, y_rows_out = sem("slot_down_ps"), sem("y_rows_ready"), sem("y_rows_out")
        picked_in = [sem(f"picked{t}_in") for t in range(T)]
        y_ready, y_out = sem("y_ready"), sem("y_out")

        LEAD = 2
        H_BANK = 0
        SHARED_BANK = 2
        SLOT_OUT_BANK, SLOT_X_BANK = 4, 5
        ROUTE_BANK, RANK_BANK = 6, 7
        ORDER = plan()

        def unit_at(n):
            return (n // J) % SHARED, n % J, n // (SHARED * J)

        block = whole.enter_context(nc.Block())

        @block.sync
        def _(sp):
            sp.dma_start(xs[:, :, :], x_d.rearrange("(t p) d -> p t d", p=P)).then_inc(x_in, 16)
            sp.dma_start(squares[:, 0:2], squares_d[:, 0:2]).then_inc(query_squares_in, 16)
            sp.dma_start(cols[:, :, :], cols_d.rearrange("(c p) n -> p c n", p=P)).then_inc(cols_in, 16)
            for t in range(T):
                if t >= 2:
                    sp.wait_ge(scores_ps, SCH * (t - 1))
                sp.dma_start(ctxT[t % 2][:, :, :, :],
                             ctxT_d[2 * t:2 * t + 2].rearrange("b (c p) k -> p b c k", p=P)
                             ).then_inc(ctxT_in[t % 2], 16)
                if t == 0:
                    sp.dma_start(squares[:, 2:7], squares_d[:, 2:7]).then_inc(squares_in, 16)
                    sp.dma_start(rows[:, :], rows_d.partition_broadcast(P)).then_inc(rows_in, 16)
                if t >= 2:
                    sp.wait_ge(pv_ps, t - 1)
                for b in range(2):
                    sp.dma_start(ctx[t % 2][:, b, 0:KT - 1, :],
                                 ctx_d[2 * t + b, 0:(KT - 1) * P].rearrange("(k p) d -> p k d", p=P)
                                 ).then_inc(ctx_in[t % 2], 16)
                    sp.dma_start(ctx[t % 2][0:KREM, b, KT - 1, :],
                                 ctx_d[2 * t + b, (KT - 1) * P:KV]).then_inc(ctx_in[t % 2], 16)
            sp.wait_ge(consts, 7)
            sp.dma_start(slot_x_d.rearrange("(s p) d -> p s d", p=P),
                         zeros[:, :].unsqueeze(1).to_broadcast([P, SLOTS, D])).then_inc(slots_zeroed, 16)
            sp.dma_start(raw[0][:, :, :], experts_d[0]).then_inc(raw_in[0], 16)
            sp.wait_ge(pv_ps, T - 1)
            sp.wait_ge(scores_ps, SCH * (T - 1))
            sp.dma_start(raw[1][:, :, :], experts_d[1]).then_inc(raw_in[1], 16)
            sp.wait_ge(wlo_ready, J)
            sp.dma_start(raw[0][:, :, :], experts_d[SHARED]).then_inc(raw_in[0], 16)
            sp.wait_ge(pv_ps, T)
            sp.dma_start(raw[2][:, :, :], experts_d[SHARED + 2]).then_inc(raw_in[2], 16)
            sp.wait_ge(wlo_ready, 2 * J)
            sp.dma_start(raw[1][:, :, :], experts_d[SHARED + 1]).then_inc(raw_in[1], 16)
            sp.wait_ge(scattered, 16 * TOP * T)
            for b in range(RING):
                sp.dma_start(xrow[:, b, :], slot_x_d[b * P:(b + 1) * P, :]).then_inc(xrow_in[b], 16)
            sp.wait_ge(expert_ready, 1)
            slots_x = slot_x_d.rearrange("(s p) d -> p s d", p=P)
            with sp.Fori(1, SLOTS // RING) as i:
                for b in range(RING):
                    slot = i * RING + b
                    expert = sp.value_load(expert_of[0:1, bass.ds(slot, 1)], min_val=0, max_val=ROUTED - 1)
                    sp.wait_ge(xrowT_ps, slot - RING + 1)
                    sp.dma_start(xrow[:, b, :], slots_x[:, bass.ds(slot, 1), :].rearrange("p s d -> p (s d)")
                                 ).then_inc(xrow_in[b], 16)
                    sp.wait_ge(slot_down_ps, slot - RING + 1)
                    sp.dma_start(raw[b][:, :, :],
                                 experts_d[bass.ds(expert + SHARED, 1)].rearrange("e p j w -> p (e j) w")
                                 ).then_inc(raw_in[b], 16)
            sp.wait_ge(y_ready, T)
            sp.dma_start(out_d.rearrange("(t p) d -> p t d", p=P), xs[:, :, :]).then_inc(y_out, 16)
            sp.wait_ge(y_out, 16)

        @block.gpsimd
        def _(pool):
            own = [0]

            def link(ins):
                own[0] += 1
                ins.then_inc(pool_own, 1)
                pool.wait_ge(pool_own, own[0])

            pool.memset(neghalf[:, :], -0.5).then_inc(consts, 1)
            link(pool.memset(ident[:, :], 0.0))
            pool.affine_select(out=ident[:, :], in_=ident[:, :], compare_op=ALU.not_equal, fill=1.0, base=0,
                               pattern=[[-1, P]], channel_multiplier=1).then_inc(consts, 1)
            pool.memset(ones[:, :], 1.0).then_inc(consts, 1)
            link(pool.memset(mask[:, :], 0.0))
            link(pool.affine_select(out=mask[:, :], in_=mask[:, :], compare_op=ALU.is_ge, fill=MASKED, base=0,
                                    pattern=[[-1, P]], channel_multiplier=1))
            pool.memset(mask[SQ:P, 0:SQ], MASKED).then_inc(consts, 1)
            pool.wait_ge(consts, 4)
            link(pool.memset(tri[:, :], 1.0))
            pool.affine_select(out=tri[:, :], in_=tri[:, :], compare_op=ALU.is_ge, fill=0.0, base=-1,
                               pattern=[[1, P]], channel_multiplier=-1).then_inc(consts, 1)
            pool.memset(zeros[:, :], 0.0).then_inc(consts, 1)
            pool.wait_ge(consts, 6)
            link(pool.iota(iota128[:, :], pattern=[[P, ROUTED]], base=0, channel_multiplier=0,
                           allow_small_or_imprecise_dtypes=True))
            link(pool.iota(over_no[:, :, :], pattern=[[1, OVER], [0, ROUTED]], base=0, channel_multiplier=0,
                           allow_small_or_imprecise_dtypes=True))
            link(pool.iota(expert_f[:, :], pattern=[[1, SLOTS]], base=0, channel_multiplier=0,
                           allow_small_or_imprecise_dtypes=True))
            link(pool.memset(before[:, 0, :], 0.0))
            link(pool.memset(ones8[:, :], 1.0))
            pool.iota(iota8[:, :, :], pattern=[[0, T], [1, ROUTED]], base=0, channel_multiplier=0,
                      allow_small_or_imprecise_dtypes=True).then_inc(consts, 1)
            pool.wait_ge(consts, 7)
            pool.wait_ge(var_ready, 1)
            pool.tensor_tensor(rstd[:, :], veps[:, :], neghalf[:, :], ALU.pow).then_inc(rstd_ready, 1)
            for t in range(T):
                for norm in range(2):
                    pool.wait_ge(var_ready, 2 + 2 * t + norm)
                    pool.tensor_tensor(rstd[:, t:t + 1], veps[:, t:t + 1], neghalf[:, t:t + 1], ALU.pow
                                       ).then_inc(rstd_ready, 1)
            pool.wait_ge(slots_zeroed, 16)
            pool.wait_ge(rows_of_ready, 1)
            for k in range(TOP):
                for t in range(T):
                    pool.indirect_dma_start(out=slot_x_d,
                                            out_offset=bass.IndirectOffsetOnAxis(ap=rows_of[:, k, t:t + 1], axis=0),
                                            in_=xn[:, t, :], in_offset=None).then_inc(scattered, 16)
            pool.wait_ge(y_rows_out, 16 * SLOTS)
            for t in range(T):
                for k in range(TOP):
                    pool.indirect_dma_start(out=picked[:, k, t, :], out_offset=None, in_=slot_y_d,
                                            in_offset=bass.IndirectOffsetOnAxis(ap=rows_of[:, k, t:t + 1], axis=0)
                                            ).then_inc(picked_in[t], 16)

        @block.tensor
        def _(pe):
            def mm(out, lhsT, rhs, first, last):
                return pe.matmul(out, lhsT, rhs, start=first, stop=last)

            def fold(b, left, right):
                for m in range(C):
                    for k in range(C):
                        ins = mm(bank(b, m * D, D), squares[:, left, k, m * P:(m + 1) * P],
                                 squares[:, right, k, :], k == 0, k == C - 1)
                ins.then_inc(fold_ps, 1)

            def fold_vec(at, left, col):
                for m in range(C):
                    for k in range(C):
                        ins = mm(bank(3, D + at + m, 1), squares[:, left, k, m * P:(m + 1) * P],
                                 cols[:, k, col:col + 1], k == 0, k == C - 1)
                return ins

            def fold_dot(at, spread, col):
                for k in range(C):
                    ins = mm(bank(3, D + at, 1), bcast[:, spread, k, :], cols[:, k, col:col + 1],
                             k == 0, k == C - 1)
                return ins

            pe.wait_ge(query_squares_in, 16)
            fold(0, XWQT, XWKT)
            pe.wait_ge(cols_in, 16)
            fold_vec(0, XWKT, XBQ)
            fold_vec(2, XWQT, XBK)
            pe.wait_ge(bcast_ready, 3)
            fold_dot(4, 0, XBK).then_inc(fold_ps, 1)
            pe.wait_ge(consts, 7)
            pe.wait_ge(xn1_ready, T)
            for t in range(T):
                for c in range(C):
                    ins = pe.transpose(bank(PT + t // 2, (t % 2) * D + c * P, P),
                                       xn[:, t, c * P:(c + 1) * P], ident[:, :])
                if t % 2 == 1:
                    ins.then_inc(xT_ps, 1)
            pe.wait_ge(fold_act, 1)
            pe.wait_ge(fold_dve, 1)
            for t in range(T):
                pe.wait_ge(xT_sb, t // 2 + 1)
                tok = slice(t * P, (t + 1) * P)
                for m in range(C):
                    for k in range(C):
                        ins = mm(bank(PO + t // 2, (t % 2) * D + m * P, P), aq[:, k, m * P:(m + 1) * P],
                                 xT[:, k, tok], k == 0, k == C - 1)
                if t % 2 == 1:
                    ins.then_inc(q_ps, 1)
            for t in range(T):
                for k in range(C):
                    ins = mm(bank(0, t, 1), xT[:, k, t * P:(t + 1) * P], vecs[:, 2 + k:3 + k],
                             k == 0, k == C - 1)
            ins.then_inc(cq_ps, 1)

            def scores(t, ch):
                if t == 0 and ch == 0:
                    pe.wait_ge(q_sb, 2)
                    pe.wait_ge(cq_sb, 1)
                if ch == 0:
                    pe.wait_ge(ctxT_in[t % 2], 16 * (t // 2 + 1))
                if t >= 1:
                    pe.wait_ge(exp_done, SCH * (t - 1) + ch + 1)
                s = scols(ch)
                for c in range(C):
                    for b in range(2):
                        ins = mm(psum[b * SQ:(b + 1) * SQ, s], qT[:, c, t * P + b * SQ:t * P + (b + 1) * SQ],
                                 ctxT[t % 2][:, b, c, s], c == 0, c == C - 1)
                ins.then_inc(scores_ps, 1)

            def transpose_probs(t, g):
                if g == 0:
                    pe.wait_ge(exp_done, SCH * (t + 1))
                if g == 0 and t >= 1:
                    pe.wait_ge(probT_act, 3 * t - 1)
                elif g == 1 and t >= 1:
                    pe.wait_ge(probT_act, 3 * t)
                elif g == 2:
                    pe.wait_ge(probT_act, 3 * t + 1)
                elif g == 3:
                    pe.wait_ge(probT_dve, t + 1)
                for k in range(4 * g, min(4 * g + 4, KT)):
                    r = P if k < KT - 1 else KREM
                    ins = pe.transpose(bank(PT + g % 2, (k % 4) * P, P)[0:r, :],
                                       prob[:, k * P:k * P + r], ident[:, :])
                ins.then_inc(probT_ps, 1)

            def weigh(t, k0, k1):
                if k0 == 0:
                    pe.wait_ge(ctx_in[t % 2], 64 * (t // 2 + 1))
                    pe.wait_ge(probT_act, 3 * (t + 1))
                    pe.wait_ge(probT_dve, t + 1)
                    if t >= 1:
                        pe.wait_ge(mix_ready, t)
                for k in range(k0, k1):
                    r = P if k < KT - 1 else KREM
                    for b in range(2):
                        ins = mm(bank(PO, 0, D)[b * SQ:(b + 1) * SQ, :], probT[0:r, k, b * SQ:(b + 1) * SQ],
                                 ctx[t % 2][0:r, b, k, :], k == 0, k == KT - 1)
                if k1 == KT:
                    ins.then_inc(pv_ps, 1)

            def chain_mixT(t):
                pe.wait_ge(mix_ready, t + 1)
                if 1 <= t < T - 1:
                    pe.wait_ge(xn3T_sb, t)
                for c in range(C):
                    ins = pe.transpose(bank(chain_bank(t), c * P, P), mix[:, c * P:(c + 1) * P], ident[:, :])
                ins.then_inc(mixT_ps, 1)

            def chain_proj(t):
                pe.wait_ge(mixT_sb, t + 1)
                if t == 0:
                    pe.wait_ge(fold_act, 2)
                for c in range(C):
                    ins = mm(bank(chain_bank(t), 0, D), mixT[:, c, :], wvo[:, c, :], c == 0, c == C - 1)
                ins.then_inc(proj_ps, 1)

            def chain_xn2T(t):
                pe.wait_ge(xn2_ready, t + 1)
                for c in range(C):
                    ins = pe.transpose(bank(chain_bank(t), c * P, P), xn[:, t, c * P:(c + 1) * P], ident[:, :])
                ins.then_inc(xn2T_ps, 1)

            def chain_tq(t):
                pe.wait_ge(xn2T_sb, t + 1)
                if t == 0:
                    pe.wait_ge(fold_act, 3)
                    pe.wait_ge(fold_dve, 3)
                for m in range(C):
                    for k in range(C):
                        mm(bank(chain_bank(t), m * P, P), a2[:, k, m * P:(m + 1) * P], xn2T[:, k, :],
                           k == 0, k == C - 1)
                for k in range(C):
                    ins = mm(bank(chain_bank(t), D, 1), xn2T[:, k, :], vecs[:, 7 + k:8 + k], k == 0, k == C - 1)
                ins.then_inc(tq_ps, 1)

            def chain_scores(t):
                pe.wait_ge(tq_sb, C * (t + 1))
                pe.wait_ge(c2_sb, t + 1)
                for c in range(C):
                    ins = mm(bank(chain_bank(t), 0, P), tq[:, c, :], xn2T[:, c, :], c == 0, c == C - 1)
                ins.then_inc(sc2_ps, 1)

            def chain_v(t):
                pe.wait_ge(sm_ready, t + 1)
                for c in range(C):
                    ins = mm(bank(chain_bank(t), 0, D), xn2T[:, c, :], squares[:, AWVT, c, :], c == 0, c == C - 1)
                ins.then_inc(v_ps, 1)

            def chain_prob2T(t):
                pe.wait_ge(prob2_ready, t + 1)
                pe.wait_ge(v_sb, t + 1)
                pe.transpose(bank(chain_bank(t), 0, P), prob2[:, :], ident[:, :]).then_inc(prob2T_ps, 1)

            def chain_z(t):
                pe.wait_ge(prob2T_sb, t + 1)
                mm(bank(chain_bank(t), 0, D), prob2T[:, :], v2[:, :], True, True).then_inc(z_ps, 1)

            def chain_xn3T(t):
                pe.wait_ge(xn3_ready, t + 1)
                for c in range(C):
                    ins = pe.transpose(bank(chain_bank(t), c * P, P), xn[:, t, c * P:(c + 1) * P], ident[:, :])
                ins.then_inc(xn3T_ps, 1)

            for ch in range(SCH):
                scores(0, ch)
            pe.wait_ge(squares_in, 16)
            for m in range(C):
                for k in range(C):
                    ins = mm(bank(PT, m * D, D), squares[:, XWVT, k, m * P:(m + 1) * P],
                             squares[:, XWO, k, :], k == 0, k == C - 1)
            ins.then_inc(fold_ps, 1)
            for m in range(C):
                for k in range(C):
                    ins = mm(bank(PT + 1, m * D, D), squares[:, AWQ, k, m * P:(m + 1) * P],
                             squares[:, AWK, k, :], k == 0, k == C - 1)
            ins.then_inc(fold_ps, 1)
            for k in range(C):
                mm(bank(PO, 0, D), bcast[:, 1, k, :], squares[:, XWO, k, :], k == 0, k == C - 1)
            for m in range(C):
                for k in range(C):
                    mm(bank(PO, D + m, 1), squares[:, AWK, k, m * P:(m + 1) * P],
                       cols[:, k, ABQ:ABQ + 1], k == 0, k == C - 1)
                for k in range(C):
                    mm(bank(PO, D + 2 + m, 1), squares[:, AWQ, k, m * P:(m + 1) * P],
                       cols[:, k, ABK:ABK + 1], k == 0, k == C - 1)
            for k in range(C):
                ins = mm(bank(PO, D + 4, 1), bcast[:, 2, k, :], cols[:, k, ABK:ABK + 1], k == 0, k == C - 1)
            ins.then_inc(fold_ps, 1)
            pe.wait_ge(fold_act, 3)
            pe.wait_ge(fold_dve, 3)
            def route():
                pe.wait_ge(xn3T_sb, T)
                for t in range(T):
                    for c in range(C):
                        ins = mm(bank(ROUTE_BANK, t * ROUTED, ROUTED), xT[:, c, t * P:(t + 1) * P],
                                 cols[:, c, CENT:CENT + ROUTED], c == 0, c == C - 1)
                ins.then_inc(route_ps, 1)

            def ranks():
                pe.wait_ge(chosen_ready, 1)
                mm(bank(RANK_BANK, 0, T * ROUTED), tri[:, :], chosen[:, :, :].rearrange("p t e -> p (t e)"),
                   True, False)
                mm(bank(RANK_BANK, 0, T * ROUTED), ones[:, :], before[:, :, :].rearrange("p t e -> p (t e)"),
                   False, True)
                mm(bank(RANK_BANK, T * ROUTED, ROUTED), ones[:, :], total[:, :], True, True).then_inc(rank_ps, 1)

            def hidden(s, w, tok):
                j = s % J
                h = bank(H_BANK + s % 2, 0, tok.stop - tok.start)
                parts = ((whi, xh), (whi, xl), (wlo, xh))
                for c in range(C):
                    for n, (wp, xp) in enumerate(parts):
                        ins = mm(h, wp[w][:, j, c * P:(c + 1) * P], xp[:, c, tok],
                                 c == 0 and n == 0, c == C - 1 and n == len(parts) - 1)
                ins.then_inc(hidden_ps, 1)

            def unit_down(n):
                e, j, half = unit_at(n)
                for p, (hp, wp) in enumerate(((hhi, whi), (hhi, wlo), (hlo, whi))):
                    for tile in range(2):
                        first = (e, j, p, tile) == (0, 0, 0, 0)
                        last = (e, j, p) == (SHARED - 1, J - 1, 2)
                        ins = pe.matmul(bank(SHARED_BANK + half, tile * D, D),
                                        hp[:, n % 2, tile * P:(tile + 1) * P], wp[e][:, j, C * P:STEP_W],
                                        start=first, stop=last, skip_group_check=True)
                ins.then_inc(down_ps, 1)

            def unit_hidden(n):
                if n >= 2:
                    pe.wait_ge(gelu_done, n - 1)
                e, j, half = unit_at(n)
                pe.wait_ge(xl_ready, 2 * (half + 1))
                pe.wait_ge(wlo_ready, J * e + j + 1)
                hidden(n, e, slice(half * HALF, (half + 1) * HALF))

            def unit(n):
                pe.wait_ge(hlo_ready, n + 1)
                unit_down(n)
                if n + LEAD < UNITS:
                    unit_hidden(n + LEAD)

            mine = {"T": transpose_probs, "S": scores, "W": weigh, "mixT": chain_mixT, "proj": chain_proj,
                    "xn2T": chain_xn2T, "tq": chain_tq, "sc": chain_scores, "v": chain_v,
                    "probT": chain_prob2T, "z": chain_z, "xn3T": chain_xn3T, "lead": unit_hidden,
                    "unit": unit, "route": route, "rank": ranks}
            for what, *args in ORDER:
                if what in mine:
                    mine[what](*args)

            def slot_rows(b, n):
                pe.wait_ge(xrow_in[b], 16 * n)
                for c in range(C):
                    ins = pe.transpose(bank(SLOT_X_BANK, c * P, P), xrow[:, b, c * P:(c + 1) * P], ident[:, :])
                ins.then_inc(xrowT_ps, 1)

            def turn(i, last):
                for b in range(RING):
                    slot = i * RING + b
                    pe.wait_ge(raw_in[b], 16 * (i + (2 if b < 2 else 1)))
                    pe.wait_ge(xrowT_sb, slot + 1)
                    for half in range(2):
                        for j in range(4 * half, 4 * half + 4):
                            for c in range(C):
                                ins = mm(bank(H_BANK + half, (j % 4) * P, P), raw[b][:, j, c * P:(c + 1) * P],
                                         xrowT[:, c, :], c == 0, c == C - 1)
                        ins.then_inc(slot_hidden_ps, 1)
                    if not last or b + 1 < RING:
                        slot_rows((b + 1) % RING, i + 1 + (b + 1) // RING)
                    pe.wait_ge(y_rows_ready, slot + 1)
                    for j in range(J):
                        if j % 4 == 0:
                            pe.wait_ge(slot_gelu, 2 * slot + j // 4 + 1)
                        ins = mm(bank(SLOT_OUT_BANK, 0, D), hT[:, j // 4, (j % 4) * P:(j % 4 + 1) * P],
                                 raw[b][:, j, C * P:STEP_W], j == 0, j == J - 1)
                    ins.then_inc(slot_down_ps, 1)

            slot_rows(0, 1)
            pe.wait_ge(gelu_done, UNITS)
            with pe.Fori(0, SLOTS // RING - 1) as i:
                turn(i, False)
            turn(SLOTS // RING - 1, True)

        @block.scalar
        def _(act):
            act.wait_ge(fold_ps, 1)
            act.activation(aq[:, :, :].rearrange("p c d -> p (c d)"), bank(0), ACT.Copy, scale=SCALE
                           ).then_inc(fold_act, 1)
            for h in range(2):
                act.wait_ge(xT_ps, h + 1)
                act.activation(xT[:, :, 2 * h * P:2 * (h + 1) * P].rearrange("p c (t n) -> p t c n", t=2),
                               bank(PT + h).rearrange("p (t c n) -> p t c n", t=2, c=C), ACT.Copy
                               ).then_inc(xT_sb, 1)
            act.wait_ge(fold_dve, 1)
            for h in range(2):
                act.wait_ge(q_ps, h + 1)
                for c in range(C):
                    ins = act.activation(qT[:, c, 2 * h * P:2 * (h + 1) * P].rearrange("p (t n) -> p t n", t=2),
                                         bank(PO + h).rearrange("p (t c n) -> p t c n", t=2, c=C)[:, :, c, :],
                                         ACT.Identity, bias=vecs[:, c:c + 1])
                ins.then_inc(q_sb, 1)
            def exps(t, ch):
                act.wait_ge(nb_ready, t + 1)
                s = scols(ch)
                act.activation(prob[:, s], psum[:, s], ACT.Exp, bias=nb[:, :], accum_out=lsum[:, t % 2, ch:ch + 1]
                               ).then_inc(exp_done, 1)

            def probT_copy(t, g):
                if g == 1:
                    return
                act.wait_ge(probT_ps, TG * t + g + 1)
                if g == TG - 1:
                    ins = act.activation(probT[0:KREM, KT - 1, :], bank(PT + g % 2, 0, P)[0:KREM, :], ACT.Copy)
                else:
                    ins = act.activation(probT[:, 4 * g:4 * g + 4, :].rearrange("p k n -> p (k n)"),
                                         bank(PT + g % 2), ACT.Copy)
                ins.then_inc(probT_act, 1)

            def xn2T_copy(t):
                act.wait_ge(xn2T_ps, t + 1)
                act.activation(xn2T[:, :, :].rearrange("p c n -> p (c n)"), bank(chain_bank(t), 0, D), ACT.Copy
                               ).then_inc(xn2T_sb, 1)

            def tq_copy(t):
                act.wait_ge(tq_ps, t + 1)
                for c in range(C):
                    act.activation(tq[:, c, :], bank(chain_bank(t), c * P, P), ACT.Identity, bias=vecs[:, 5 + c:6 + c]
                                   ).then_inc(tq_sb, 1)

            def exp2(t):
                act.wait_ge(nb2_ready, t + 1)
                act.activation(prob2[:, :], sm[:, :], ACT.Exp, bias=nb2[:, :], accum_out=lsum2[:, :]
                               ).then_inc(prob2_ready, 1)

            def prob2T_copy(t):
                act.wait_ge(prob2T_ps, t + 1)
                act.activation(prob2T[:, :], bank(chain_bank(t), 0, P), ACT.Copy).then_inc(prob2T_sb, 1)

            def xn3T_copy(t):
                tok = slice(t * P, (t + 1) * P)
                act.wait_ge(xn3T_ps, t + 1)
                act.activation(xT[:, :, tok], bank(chain_bank(t), 0, D).rearrange("p (c n) -> p c n", c=C), ACT.Copy
                               ).then_inc(xn3T_sb, 1)
                act.wait_ge(xn3T_sb, t + 1)
                act.activation(xh[:, :, tok], xT[:, :, tok], ACT.Copy).then_inc(xh_ready, 1)

            def split_high(j, w):
                act.activation(whi[w][:, j, :], raw[w][:, j, :], ACT.Copy).then_inc(whi_ready, 1)

            def split(q):
                e, j = q // J, q % J
                if j == 0:
                    act.wait_ge(raw_in[e % 2], 16 * (e // 2 + 1))
                if q == 0:
                    act.wait_ge(pv_ps, T - 1)
                if q == J:
                    act.wait_ge(pv_ps, T)
                split_high(j, e % 2)

            def stage(n):
                act.wait_ge(hidden_ps, n + 1)
                if n >= 2:
                    act.wait_ge(hlo_ready, n - 1)
                act.activation(hraw[:, n % 2, :], bank(H_BANK + n % 2, 0, HALF), ACT.Gelu).then_inc(gelu_done, 1)
                act.wait_ge(gelu_done, n + 1)
                if n >= 2:
                    act.wait_ge(down_ps, n - 1)
                act.activation(hhi[:, n % 2, :], hraw[:, n % 2, :], ACT.Copy).then_inc(hhi_ready, 1)

            def unit(n):
                if n + LEAD < UNITS:
                    stage(n + LEAD)

            def route():
                act.wait_ge(rz_ready, 2)
                act.activation(sg[:, :, :, :].rearrange("p a t e -> p (a t e)"),
                               rz[:, :, :, :].rearrange("p a t e -> p (a t e)"), ACT.Exp, scale=-1.0
                               ).then_inc(sig_ready, 1)

            def gates():
                act.wait_ge(gap_ready, 1)
                act.activation(gap[:, :], gap[:, :], ACT.Tanh, scale=0.5).then_inc(tanh_done, 1)

            for ch in range(SCH):
                exps(0, ch)
            act.wait_ge(fold_ps, 3)
            act.activation(wvo[:, :, :].rearrange("p c d -> p (c d)"), bank(PT), ACT.Copy).then_inc(fold_act, 1)
            act.wait_ge(fold_ps, 4)
            act.activation(a2[:, :, :].rearrange("p c d -> p (c d)"), bank(PT + 1), ACT.Copy, scale=SCALE
                           ).then_inc(fold_act, 1)
            mine = {"T": probT_copy, "exp": exps, "xn2T": xn2T_copy, "tq": tq_copy, "sc": exp2,
                    "probT": prob2T_copy, "xn3T": xn3T_copy, "split": split, "unit": unit,
                    "lead": stage, "route": route, "gates": gates}
            for what, *args in ORDER:
                if what in mine:
                    mine[what](*args)

            slots_y = slot_y_d.rearrange("(s p) d -> p s d", p=P)
            with act.Fori(0, SLOTS // RING) as i:
                for b in range(RING):
                    slot = i * RING + b
                    for half in range(2):
                        act.wait_ge(slot_hidden_ps, 2 * slot + half + 1)
                        act.activation(hT[:, half, :], bank(H_BANK + half), ACT.Gelu).then_inc(slot_gelu, 1)
                    act.wait_ge(y_rows_ready, slot + 2)
                    act.dma_start(slots_y[:, bass.ds(slot, 1), :], y_rows[:, bass.ds(slot, 1), :]
                                  ).then_inc(y_rows_out, 16)

        @block.vector
        def _(dve):
            own = [0]

            def link(ins):
                own[0] += 1
                ins.then_inc(dve_own, 1)
                dve.wait_ge(dve_own, own[0])

            def norm(t, ready):
                link(dve.bn_stats(stats[:, t, :], xs[:, t, :]))
                link(dve.bn_aggr(mv[:, t, :], stats[:, t, :]))
                dve.tensor_scalar(veps[:, t:t + 1], mv[:, t, 1:2], EPS, None, ALU.add).then_inc(var_ready, 1)
                dve.wait_ge(rstd_ready, ready)
                return dve.tensor_scalar(xn[:, t, :], xs[:, t, :], mv[:, t, 0:1], rstd[:, t:t + 1],
                                         ALU.subtract, ALU.mult)

            dve.wait_ge(x_in, 16)
            for t in range(T):
                ins = dve.bn_stats(stats[:, t, :], xs[:, t, :])
            link(ins)
            for t in range(T):
                ins = dve.bn_aggr(mv[:, t, :], stats[:, t, :])
            link(ins)
            dve.tensor_scalar(veps[:, :], mv[:, :, 1], EPS, None, ALU.add).then_inc(var_ready, 1)
            dve.wait_ge(consts, 7)
            dve.wait_ge(cols_in, 16)
            for n, col in enumerate((XBQ, XBV, ABQ)):
                for c in range(C):
                    ins = dve.tensor_scalar(bcast[:, n, c, :], ones[:, :], cols[:, c, col:col + 1], None, ALU.mult)
                ins.then_inc(bcast_ready, 1)
            dve.wait_ge(rstd_ready, 1)
            for t in range(T):
                dve.tensor_scalar(xn[:, t, :], xs[:, t, :], mv[:, t, 0:1], rstd[:, t:t + 1],
                                  ALU.subtract, ALU.mult).then_inc(xn1_ready, 1)
            dve.wait_ge(fold_ps, 2)
            dve.tensor_scalar(vecs[:, 0:5], bank(3, D, 5), SCALE, None, ALU.mult).then_inc(fold_dve, 1)
            dve.wait_ge(fold_dve, 1)
            dve.wait_ge(cq_ps, 1)
            dve.tensor_scalar(cq[:, :], bank(0, 0, T), vecs[:, 4:5], None, ALU.add).then_inc(cq_sb, 1)

            def max_chunk(t, ch):
                dve.wait_ge(scores_ps, SCH * t + ch + 1)
                ins = dve.tensor_reduce(cmax[:, ch:ch + 1], psum[:, scols(ch)], AX_X, ALU.max)
                if ch == SCH - 1:
                    link(ins)
                    link(dve.tensor_reduce(small[:, 0:1], cmax[:, :], AX_X, ALU.max))
                    link(dve.tensor_tensor(small[:, 1:2], small[:, 0:1], cq[:, t:t + 1], ALU.add))
                    if t >= 1:
                        dve.wait_ge(exp_done, SCH * t)
                    dve.tensor_tensor(nb[:, :], cq[:, t:t + 1], small[:, 1:2], ALU.subtract).then_inc(nb_ready, 1)

            for ch in range(SCH):
                max_chunk(0, ch)
            dve.wait_ge(fold_ps, 5)
            dve.wait_ge(rows_in, 16)
            dve.tensor_tensor(mix[:, :], bank(PO, 0, D), rows[:, 0:D], ALU.add).then_inc(fold_dve, 1)
            dve.tensor_scalar(vecs[:, 5:10], bank(PO, D, 5), SCALE, None, ALU.mult).then_inc(fold_dve, 1)
            dve.wait_ge(fold_dve, 2)
            for t in range(T):
                ins = dve.tensor_tensor(xs[:, t, :], xs[:, t, :], mix[:, :], ALU.add)
            link(ins)

            def probT_copy(t, g):
                if g == 1:
                    dve.wait_ge(probT_ps, TG * t + g + 1)
                    dve.tensor_copy(probT[:, 4 * g:4 * g + 4, :].rearrange("p k n -> p (k n)"),
                                    bank(PT + g % 2)).then_inc(probT_dve, 1)

            def mix_scale(t):
                dve.wait_ge(exp_done, SCH * (t + 1))
                link(dve.tensor_reduce(small[:, 2:3], lsum[:, t % 2, :], AX_X, ALU.add))
                link(dve.reciprocal(linv[:, 0:1], small[:, 2:3]))
                dve.wait_ge(pv_ps, t + 1)
                dve.tensor_scalar(mix[:, :], bank(PO, 0, D), linv[:, 0:1], None, ALU.mult).then_inc(mix_ready, 1)

            def mixT_copy(t):
                dve.wait_ge(mixT_ps, t + 1)
                dve.tensor_copy(mixT[:, :, :].rearrange("p c n -> p (c n)"), bank(chain_bank(t), 0, D)
                                ).then_inc(mixT_sb, 1)

            def x1_add(t):
                dve.wait_ge(proj_ps, t + 1)
                dve.tensor_tensor(xs[:, t, :], bank(chain_bank(t), 0, D), xs[:, t, :], ALU.add).then_inc(x1_ready, 1)

            def norm2(t):
                dve.wait_ge(x1_ready, t + 1)
                norm(t, 2 + 2 * t).then_inc(xn2_ready, 1)

            def c2_copy(t):
                dve.wait_ge(tq_ps, t + 1)
                dve.wait_ge(tq_sb, C * (t + 1))
                dve.tensor_scalar(c2[:, :], bank(chain_bank(t), D, 1), vecs[:, 9:10], None, ALU.add).then_inc(c2_sb, 1)

            def softmax2(t):
                dve.wait_ge(sc2_ps, t + 1)
                dve.wait_ge(c2_sb, t + 1)
                dve.tensor_tensor(sm[:, :], bank(chain_bank(t), 0, P), mask[:, :], ALU.add).then_inc(sm_ready, 1)
                dve.wait_ge(sm_ready, t + 1)
                link(dve.tensor_reduce(small2[:, 0:1], sm[:, :], AX_X, ALU.max))
                link(dve.tensor_tensor(small2[:, 1:2], small2[:, 0:1], c2[:, :], ALU.add))
                dve.tensor_tensor(nb2[:, :], c2[:, :], small2[:, 1:2], ALU.subtract).then_inc(nb2_ready, 1)

            def v_copy(t):
                dve.wait_ge(v_ps, t + 1)
                dve.tensor_tensor(v2[:, :], bank(chain_bank(t), 0, D), rows[:, D:2 * D], ALU.add).then_inc(v_sb, 1)

            def x2_add(t):
                dve.wait_ge(prob2_ready, t + 1)
                link(dve.reciprocal(linv[:, 1:2], lsum2[:, :]))
                dve.wait_ge(z_ps, t + 1)
                dve.scalar_tensor_tensor(xs[:, t, :], bank(chain_bank(t), 0, D), linv[:, 1:2], xs[:, t, :],
                                         ALU.mult, ALU.add).then_inc(x2_ready, 1)
                dve.wait_ge(x2_ready, t + 1)
                norm(t, 3 + 2 * t).then_inc(xn3_ready, 1)
                dve.wait_ge(xn3_ready, t + 1)
                link(dve.tensor_tensor(xs[:, t, :], xs[:, t, :], xn[:, t, :], ALU.add))

            def split_x(t):
                tok = slice(t * P, (t + 1) * P)
                dve.wait_ge(xh_ready, t + 1)
                dve.tensor_tensor(xl[:, :, tok], xT[:, :, tok], xh[:, :, tok].bitcast(F32), ALU.subtract
                                  ).then_inc(xl_ready, 1)

            def x1_norm(t):
                x1_add(t)
                norm2(t)

            def weigh(t, k0, k1):
                if k1 == KT:
                    mix_scale(t)

            def split_low(q, j, w):
                dve.wait_ge(whi_ready, q + 1)
                dve.tensor_tensor(wlo[w][:, j, :], raw[w][:, j, :], whi[w][:, j, :].bitcast(F32), ALU.subtract
                                  ).then_inc(wlo_ready, 1)

            def stage(n):
                dve.wait_ge(hhi_ready, n + 1)
                dve.tensor_tensor(hlo[:, n % 2, :], hraw[:, n % 2, :], hhi[:, n % 2, :].bitcast(F32),
                                  ALU.subtract).then_inc(hlo_ready, 1)

            def unit(n):
                if n + LEAD < UNITS:
                    stage(n + LEAD)

            def route():
                dve.wait_ge(route_ps, 1)
                z = bank(ROUTE_BANK, 0, T * ROUTED).rearrange("p (t e) -> p t e", t=T)
                dve.tensor_copy(rz[:, 0, :, :], z).then_inc(rz_ready, 1)
                dve.tensor_tensor(rz[:, 1, :, :], z,
                                  rows[:, 2 * D:2 * D + ROUTED].unsqueeze(1).to_broadcast([P, T, ROUTED]),
                                  ALU.add).then_inc(rz_ready, 1)

            def top2():
                dve.wait_ge(sig_ready, 1)
                sgf = sg[:, :, :, :].rearrange("p a t e -> p (a t e)")
                link(dve.tensor_scalar(sgf, sgf, 1.0, None, ALU.add))
                link(dve.reciprocal(sgf, sgf))
                for t in range(T):
                    ins = dve.max(top8[:, t, :], sg[:, 1, t, :])
                link(ins)
                for t in range(T):
                    ins = dve.max_index(idx8[:, t, :], top8[:, t, :], sg[:, 1, t, :])
                link(ins)

            def mark():
                link(dve.tensor_copy(idxf[:, :, :], idx8[:, :, 0:TOP]))
                for k in range(TOP):
                    ins = dve.tensor_tensor(hot[:, k, :, :], iota8[:, :, :],
                                            idxf[:, :, k:k + 1].to_broadcast([P, T, ROUTED]), ALU.is_equal)
                link(ins)
                link(dve.tensor_tensor(chosen[:, :, :], hot[:, 0, :, :], hot[:, 1, :, :], ALU.add))
                for t in range(1, T):
                    link(dve.tensor_tensor(before[:, t, :], before[:, t - 1, :], chosen[:, t - 1, :], ALU.add))
                dve.tensor_tensor(total[:, :], before[:, T - 1, :], chosen[:, T - 1, :], ALU.add
                                  ).then_inc(chosen_ready, 1)

            def place():
                dve.wait_ge(rank_ps, 1)
                dve.tensor_copy(rank[:, :, :].rearrange("p t e -> p (t e)"), bank(RANK_BANK, 0, T * ROUTED))
                link(dve.tensor_copy(count[:, :], bank(RANK_BANK, T * ROUTED, ROUTED)))
                link(dve.tensor_scalar(over[:, 0, :], count[:, :], P + 0.5, None, ALU.is_gt))
                for most in (2 * P, 3 * P):
                    link(dve.scalar_tensor_tensor(over[:, 0, :], count[:, :], most + 0.5, over[:, 0, :],
                                                  ALU.is_gt, ALU.add))
                link(dve.tensor_tensor_scan(over[:, 1, :], ones8[:, :], over[:, 0, :], 0.0, ALU.mult, ALU.add))
                link(dve.tensor_tensor(over[:, 2, :], over[:, 1, :], over[:, 0, :], ALU.subtract))
                link(dve.tensor_tensor(after[:, :, :], over[:, 1, :].unsqueeze(1).to_broadcast([P, OVER, ROUTED]),
                                       over_no[:, :, :], ALU.is_le))
                link(dve.tensor_reduce(expert_f[:, ROUTED:SLOTS], after[:, :, :], AX_X, ALU.add))
                link(dve.tensor_scalar(expert_f[:, ROUTED:SLOTS], expert_f[:, ROUTED:SLOTS], ROUTED - 1.0, None,
                                       ALU.min))
                dve.tensor_copy(expert_of[:, :], expert_f[:, :]).then_inc(expert_ready, 1)
                link(dve.tensor_scalar(base[:, 0, :], over[:, 2, :], ROUTED - 1.0, float(P), ALU.add, ALU.mult))
                link(dve.tensor_tensor(base[:, 1, :], iota128[:, :], base[:, 0, :], ALU.subtract))
                link(dve.tensor_scalar(first[:, :, :], rank[:, :, :], P - 0.5, None, ALU.is_lt))
                link(dve.tensor_tensor(first[:, :, :], first[:, :, :],
                                       base[:, 1, :].unsqueeze(1).to_broadcast([P, T, ROUTED]), ALU.mult))
                link(dve.tensor_tensor(row[:, :, :], rank[:, :, :],
                                       base[:, 0, :].unsqueeze(1).to_broadcast([P, T, ROUTED]), ALU.add))
                link(dve.tensor_tensor(row[:, :, :], row[:, :, :], first[:, :, :], ALU.add))
                for k in range(TOP):
                    ins = dve.tensor_tensor(gat[:, k, :, :], hot[:, k, :, :], row[:, :, :], ALU.mult)
                link(ins)
                link(dve.tensor_reduce(rows_of_f[:, :, :], gat[:, :, :, :], AX_X, ALU.add))
                dve.tensor_copy(rows_of[:, :, :], rows_of_f[:, :, :]).then_inc(rows_of_ready, 1)

            def gates():
                dve.wait_ge(rows_of_ready, 1)
                for k in range(TOP):
                    ins = dve.tensor_tensor(gat[:, k, :, :], hot[:, k, :, :], sg[:, 0, :, :], ALU.mult)
                link(ins)
                link(dve.tensor_reduce(g2[:, :, :], gat[:, :, :, :], AX_X, ALU.add))
                dve.tensor_tensor(gap[:, :], g2[:, 0, :], g2[:, 1, :], ALU.subtract).then_inc(gap_ready, 1)
                dve.wait_ge(tanh_done, 1)
                dve.tensor_scalar(gate[:, 0, :], gap[:, :], 0.5, 0.5, ALU.mult, ALU.add)
                link(dve.tensor_scalar(gate[:, 1, :], gap[:, :], -0.5, 0.5, ALU.mult, ALU.add))

            def shared_out(half):
                dve.wait_ge(down_ps, SHARED * J * (half + 1))
                flat = xs[:, 2 * half:2 * half + 2, :].rearrange("p t d -> p (t d)")
                dve.tensor_tensor(flat, bank(SHARED_BANK + half), flat, ALU.add).then_inc(shared_read, 1)

            mine = {"T": probT_copy, "S": max_chunk, "W": weigh, "mixT": mixT_copy, "proj": x1_norm,
                    "tq": c2_copy, "sc": softmax2, "v": v_copy, "z": x2_add, "xn3T": split_x,
                    "split": lambda q: split_low(q, q % J, q // J % 2),
                    "unit": unit, "lead": stage, "route": route, "top2": top2, "hot": mark, "place": place,
                    "gates": gates, "shared_out": shared_out}
            for what, *args in ORDER:
                if what in mine:
                    mine[what](*args)

            def rows_copy(n):
                dve.wait_ge(xrowT_ps, n)
                dve.tensor_copy(xrowT[:, :, :].rearrange("p c n -> p (c n)"), bank(SLOT_X_BANK, 0, D)
                                ).then_inc(xrowT_sb, 1)

            def turn(i, last):
                for b in range(RING):
                    slot = i * RING + b
                    if not last or b + 1 < RING:
                        rows_copy(slot + 2)
                    dve.wait_ge(slot_down_ps, slot + 1)
                    dve.tensor_copy(y_rows[:, bass.ds(slot, 1), :],
                                    bank(SLOT_OUT_BANK, 0, D).unsqueeze(1)).then_inc(y_rows_ready, 1)

            dve.memset(y_rows[:, 0, :], 0.0).then_inc(y_rows_ready, 1)
            rows_copy(1)
            with dve.Fori(0, SLOTS // RING - 1) as i:
                turn(i, False)
            turn(SLOTS // RING - 1, True)
            dve.wait_ge(shared_read, 2)
            for t in range(T):
                dve.wait_ge(picked_in[t], 16 * TOP)
                link(dve.scalar_tensor_tensor(xs[:, t, :], picked[:, 0, t, :], gate[:, 0, t:t + 1], xs[:, t, :],
                                              ALU.mult, ALU.add))
                dve.scalar_tensor_tensor(xs[:, t, :], picked[:, 1, t, :], gate[:, 1, t:t + 1], xs[:, t, :],
                                         ALU.mult, ALU.add).then_inc(y_ready, 1)


def kernel(**inputs):
    import numpy as np
    import concourse.bacc as bacc
    from concourse import mybir as mb
    from concourse.bass_utils import run_bass_kernel_spmd

    a = {k: np.asarray(v) for k, v in inputs.items()}

    def up(w):
        return w.reshape(-1, J, P, C, P).transpose(0, 4, 1, 3, 2).reshape(-1, P, J, C * P)

    def down(w):
        return w.reshape(-1, D, J, P).transpose(0, 3, 2, 1)

    squares = np.stack([a["L0_xattn_Wq"].T, a["L0_xattn_Wk"].T, a["L0_xattn_Wv"].T, a["L0_xattn_Wo"],
                        a["L0_attn_Wq"], a["L0_attn_Wk"], a["L0_attn_Wv"].T])
    arrays = {
        "x_in_dram": a["x"].reshape(N, D),
        "ctx_dram": a["ctx_1024"],
        "ctxT_dram": a["ctx_1024"].transpose(0, 2, 1),
        "squares_dram": squares.reshape(7, C, P, D).transpose(2, 0, 1, 3),
        "cols_dram": np.concatenate([np.stack([a["L0_xattn_bq"], a["L0_xattn_bk"], a["L0_xattn_bv"],
                                               a["L0_attn_bq"], a["L0_attn_bk"]]),
                                     a["L0_ffn_centroids"]]).T,
        "rows_dram": np.concatenate([a["L0_xattn_bo"], a["L0_attn_bv"], a["L0_ffn_routing_bias"]]),
        "experts_dram": np.concatenate([
            np.concatenate([up(a["L0_ffn_Wfc_sh"]), down(a["L0_ffn_Wproj_sh"])], axis=3),
            np.concatenate([up(a["L0_ffn_Wfc_r"]), down(a["L0_ffn_Wproj_r"])], axis=3)]),
    }
    arrays = {k: np.ascontiguousarray(v) for k, v in arrays.items()}
    nc = bacc.Bacc("TRN2", target_bir_lowering=False, num_devices=1)
    args = [nc.dram_tensor(k, v.shape, mb.dt.from_np(v.dtype), kind="ExternalInput").ap() for k, v in arrays.items()]
    out = nc.dram_tensor("out_dram", (N, D), mb.dt.float32, kind="ExternalOutput").ap()
    slot_x = nc.dram_tensor("slot_x_dram", (SLOTS * P, D), mb.dt.float32, kind="Internal").ap()
    slot_y = nc.dram_tensor("slot_y_dram", (SLOTS * P, D), mb.dt.float32, kind="Internal").ap()
    build(nc, *args, out, slot_x, slot_y)
    r = run_bass_kernel_spmd(nc, [arrays], core_ids=[0])
    return r.results[0]["out_dram"].reshape(B, SQ, D)
```

```python
from contextlib import ExitStack

import concourse.bass as bass
from concourse import mybir

ALU = mybir.AluOpType
ACT = mybir.ActivationFunctionType
AX_X = mybir.AxisListType.X
F32 = mybir.dt.float32
F32R = mybir.dt.float32r
U32 = mybir.dt.uint32

P = 128
D = 256
C = D // P
B, SQ, KV = 8, 64, 1601
T = B // 2
N = B * SQ
F = 1024
J = F // P
SHARED, ROUTED, TOP = 2, 8, 2
KT = -(-KV // P)
KREM = KV - (KT - 1) * P
BANK = 512
SCH = -(-KV // BANK)
TG = -(-KT // 4)
STEP_W = C * P + D
EPS = 1e-5
SCALE = 1.0 / 16.0
MASKED = -3.0e38

OVER = (TOP * N - ROUTED) // P
SLOTS = ROUTED + OVER
RING = 4
LEAD = 3
HALF = N // 2
UNITS = 2 * SHARED * J

XWQT, XWKT, XWVT, XWO, AWQ, AWK, AWVT = range(7)
XBQ, XBK, XBV, ABQ, ABK, CENT = range(6)
NCOLS = CENT + ROUTED
EARLY_W = (5, 0, 0)


def scols(ch):
    return slice(ch * BANK, min(KV, (ch + 1) * BANK))


def plan():
    order = []
    for t in range(T - 1):
        c = t - 1
        chain = (lambda *names: [(name, c) for name in names]) if c >= 0 else (lambda *names: [])
        early = EARLY_W[t]
        order += [("T", t, 0), ("T", t, 1), *([("xn3T", c - 1)] if c >= 1 else []), ("T", t, 2), *chain("mixT"),
                  ("T", t, 3), *chain("proj", "norm2"), *([("x_bias", )] if t == 0 else []),
                  *([("W", t, 0, early)] if early else []),
                  ("S", t + 1, 0), *chain("xn2T"), ("S", t + 1, 1), *chain("tq"), ("S", t + 1, 2),
                  *chain("sc", "exp2"), ("S", t + 1, 3), *chain("v"), ("exp", t + 1, 0), ("exp", t + 1, 1),
                  ("W", t, early, early + 2), *chain("probT"), ("exp", t + 1, 2), ("exp", t + 1, 3),
                  ("W", t, early + 2, early + 4), *chain("z", "norm3"), ("W", t, early + 4, KT)]
    t, c = T - 1, T - 2
    order += [("T", t, 0), ("T", t, 1), ("xn3T", c - 1), ("T", t, 2), ("mixT", c), ("T", t, 3), ("proj", c),
              ("norm2", c), ("split", 0), ("W", t, 0, 3), ("split", 1), ("W", t, 3, 5), ("split", 2), ("xn2T", c),
              ("W", t, 5, 7), ("split", 3), ("tq", c), ("W", t, 7, 9), ("sc", c), ("exp2", c), ("split", 4),
              ("W", t, 9, 10), ("v", c), ("lead", 0), ("split", 5), ("W", t, 10, 11), ("lead", 1),
              ("W", t, 11, KT), ("split", 6), ("probT", c), ("lead", 2), ("split", 7), ("unit", 0),
              ("mixT", t), ("z", c), ("unit", 1),
              ("proj", t), ("norm3", c),
              ("unit", 2), ("norm2", t), ("split", 8), ("unit", 3), ("xn3T", c), ("xn2T", t),
              ("split", 9), ("unit", 4), ("tq", t), ("split", 10), ("unit", 5), ("sc", t), ("split", 11), ("unit", 6),
              ("exp2", t), ("v", t), ("unit", 7), ("split", 12), ("split", 13), ("probT", t), ("route", 0),
              ("unit", 8), ("split", 14), ("z", t), ("route", 1), ("unit", 9), ("norm3", t), ("split", 15),
              ("route", 2), ("unit", 10), ("xn3T", t), ("unit", 11), ("route", 3), ("sigmoid", ),
              ("top2", ), ("indices", ),
              ("unit", 12), ("hot", ), ("choices", ), ("unit", 13), ("unit", 14), ("unit", 15), ("rank", ),
              ("place", ), ("place_experts", ), ("unit", 16), ("place_rows", ), ("place_tokens", ),
              ("unit", 17), ("tables", ), ("unit", 18), ("gap", ), ("unit", 19), ("gates", ), ("unit", 20),
              ("unit", 21), ("unit", 22), ("unit", 23), ("shared_out", 0)]
    order += [("unit", 24), ("slot_down", 0), ("unit", 25), ("unit", 26), ("slot_down", 1), ("unit", 27),
              ("unit", 28), ("slot_rows", ), ("unit", 29), ("unit", 30), ("unit", 31), ("shared_out", 1)]
    return order


def build(nc, x_d, ctx_d, ctxT_d, squares_d, cols_d, rows_d, experts_d, out_d, slot_x_d, notes_d, results_d):
    with ExitStack() as whole:
        def sb(name, shape, dt=F32, stack=whole):
            return stack.enter_context(nc.sbuf_tensor(name, shape, dt))

        def sem(name):
            return whole.enter_context(nc.semaphore(name))

        ident = sb("ident", [P, P])
        mask = sb("mask", [P, P])
        neghalf = sb("neghalf", [P, T])
        tri = sb("tri", [P, P])
        ones = sb("ones", [P, P])
        iota8 = sb("iota8", [P, T, ROUTED])
        iota128 = sb("iota128", [P, ROUTED])
        over_no = sb("over_no", [P, OVER, ROUTED])
        zeros = sb("zeros", [P, D])
        cols = sb("cols", [P, C, NCOLS])
        rows = sb("rows", [P, 2 * D + ROUTED])
        vecs = sb("vecs", [P, 2 * C])
        xs = sb("xs", [P, T, D])
        xn = sb("xn", [P, T, D])
        xT = sb("xT", [P, C, N])
        xh = sb("xh", [P, C, N], F32R)
        xl = sb("xl", [P, C, N], F32R)
        cq = sb("cq", [P, T])
        stats = sb("stats", [P, T, 6])
        mv = sb("mv", [P, T, 2])
        veps = sb("veps", [P, T])
        rstd = sb("rstd", [P, T])
        cmax = sb("cmax", [P, SCH])
        small = sb("small", [P, 8])
        nb = sb("nb", [P, 1])
        lsum = sb("lsum", [P, 2, SCH])
        linv = sb("linv", [P, 2])
        c2 = sb("c2", [P, 1])
        small2 = sb("small2", [P, 8])
        nb2 = sb("nb2", [P, 1])
        lsum2 = sb("lsum2", [P, 1])
        rz = sb("rz", [P, 2, T, ROUTED])
        sg = sb("sg", [P, 2, T, ROUTED])
        top8 = sb("top8", [P, T, 8])
        idx8 = sb("idx8", [P, T, 8], U32)
        idxf = sb("idxf", [P, T, TOP])
        hot = sb("hot", [P, TOP, T, ROUTED])
        gat = sb("gat", [P, TOP, T, ROUTED])
        chosen = sb("chosen", [P, T, ROUTED])
        before = sb("before", [P, T, ROUTED])
        total = sb("total", [P, ROUTED])
        rank = sb("rank", [P, T, ROUTED])
        count = sb("count", [P, ROUTED])
        over = sb("over", [P, 3, ROUTED])
        ones8 = sb("ones8", [P, ROUTED])
        after = sb("after", [P, OVER, ROUTED])
        expert_f = sb("expert_f", [P, SLOTS])
        expert_of = sb("expert_of", [P, SLOTS], U32)
        base = sb("base", [P, 2, ROUTED])
        row = sb("row", [P, T, ROUTED])
        first = sb("first", [P, T, ROUTED])
        rows_of_f = sb("rows_of_f", [P, TOP, T])
        rows_of = sb("rows_of", [P, TOP, T], U32)
        g2 = sb("g2", [P, TOP, T])
        gap = sb("gap", [P, T])
        hraw = sb("hraw", [P, LEAD, HALF])
        hhi = sb("hhi", [P, LEAD, HALF], F32R)
        hlo = sb("hlo", [P, LEAD, HALF], F32R)
        notes = sb("notes", [P, TOP, T, 2])
        blank_notes = sb("blank_notes", [P, SLOTS, 2])
        slot_notes = sb("slot_notes", [P, SLOTS, 2])
        result_row = sb("result_row", [P, SLOTS], U32)

        with ExitStack() as phase1:
            sb("room_for_expert0", [P, J, STEP_W], F32, phase1)
            ctx, ctxT = [None, None], [None, None]
            for i in range(2):
                ctx[i] = sb(f"ctx{i}", [P, 2, KT, D], F32, phase1)
                ctxT[i] = sb(f"ctxT{i}", [P, 2, C, KV], F32, phase1)
            squares = sb("squares", [P, 7, C, D + 1], F32, phase1)
            aq = sb("aq", [P, C, D], F32, phase1)
            wvo = sb("wvo", [P, C, D], F32, phase1)
            a2 = sb("a2", [P, C, D], F32, phase1)
            bcast = sb("bcast", [P, 3, C, P], F32, phase1)
            wrow = sb("wrow", [P, 2, D + 1], F32, phase1)
            product = sb("product", [P, D], F32, phase1)
            qT = sb("qT", [P, C, N], F32, phase1)
            prob = sb("prob", [P, KV], F32, phase1)
            probT = sb("probT", [P, KT, P], F32, phase1)
            mix = sb("mix", [P, D], F32, phase1)
            mixT = sb("mixT", [P, C, P], F32, phase1)
            xn2T = sb("xn2T", [P, C, P], F32, phase1)
            tq = sb("tq", [P, C, P], F32, phase1)
            v2 = sb("v2", [P, D], F32, phase1)
            prob2 = sb("prob2", [P, P], F32, phase1)
            prob2T = sb("prob2T", [P, P], F32, phase1)
            sm = sb("sm", [P, P], F32, phase1)
        raw, whi, wlo = [None, None], [None, None], [None, None]
        with ExitStack() as shared_phase:
            raw[0] = sb("raw0", [P, J, STEP_W], F32, shared_phase)
            whi[0] = sb("whi0", [P, J, STEP_W], F32R, shared_phase)
            wlo[0] = sb("wlo0", [P, J, STEP_W], F32R, shared_phase)
            raw[1] = sb("raw1", [P, J, STEP_W], F32, shared_phase)
            whi[1] = sb("whi1", [P, J, STEP_W], F32R, shared_phase)
            wlo[1] = sb("wlo1", [P, J, STEP_W], F32R, shared_phase)
        ring, dhi, dlo = [None] * RING, [None, None], [None, None]
        ring[0] = sb("ring0", [P, J, STEP_W])
        dhi[1] = sb("dhi1", [P, J, D], F32R)
        dlo[1] = sb("dlo1", [P, J, D], F32R)
        xrow = sb("xrow", [P, RING, D])
        slot_h = sb("slot_h", [P, 2, BANK])
        slot_hhi = sb("slot_hhi", [P, 2, BANK], F32R)
        slot_hlo = sb("slot_hlo", [P, 2, BANK], F32R)
        ring[1] = sb("ring1", [P, J, STEP_W])
        picked = sb("picked", [P, TOP, T, D])
        y_rows = sb("y_rows", [P, SLOTS, D])
        sb("rest_of_wlo1", [P, (2 * J * STEP_W - TOP * N // P * D) // D - SLOTS, D])
        ring[2] = sb("ring2", [P, J, STEP_W])
        ring[3] = sb("ring3", [P, J, STEP_W])
        dhi[0] = sb("dhi0", [P, J, D], F32R)
        dlo[0] = sb("dlo0", [P, J, D], F32R)
        xrowT = sb("xrowT", [P, C, P])

        psum = whole.enter_context(nc.psum_tensor("psum", [P, 8 * BANK], F32))

        def bank(b, lo=0, n=BANK):
            return psum[:, b * BANK + lo:b * BANK + lo + n]

        PT = 4
        PO = 6
        CHAIN = 7

        def chain_bank(t):
            return CHAIN if t < T - 1 else PT + 1

        x_in, query_squares_in, squares_in, cols_in, rows_in = (
            sem("x_in"), sem("query_squares_in"), sem("squares_in"), sem("cols_in"), sem("rows_in"))
        ctx_in = [sem("ctx0_in"), sem("ctx1_in")]
        ctxT_in = [[sem("ctxT0_start_in"), sem("ctxT0_rest_in")], [sem("ctxT1_start_in"), sem("ctxT1_rest_in")]]
        raw_in = [sem("raw0_in"), sem("raw1_in")]
        ring_in = [sem(f"ring{b}_in") for b in range(RING)]
        xrow_in, notes_in = [sem(f"xrow{b}_in") for b in range(RING)], sem("notes_in")
        consts = sem("consts")
        pool_own, dve_own = sem("pool_own"), sem("dve_own")
        bcast_ready = sem("bcast_ready")
        fold_ps, fold_act, fold_dve = sem("fold_ps"), sem("fold_act"), sem("fold_dve")
        var_ready, rstd_ready = sem("var_ready"), sem("rstd_ready")
        xn1_ready, xT_ps, xT_sb, q_ps, q_sb = (
            sem("xn1_ready"), sem("xT_ps"), sem("xT_sb"), sem("q_ps"), sem("q_sb"))
        scores_ps, nb_ready, exp_done = sem("scores_ps"), sem("nb_ready"), sem("exp_done")
        probT_ps, probT_act, probT_dve = sem("probT_ps"), sem("probT_act"), sem("probT_dve")
        pv_ps, mix_ready, mixT_ps, mixT_sb = sem("pv_ps"), sem("mix_ready"), sem("mixT_ps"), sem("mixT_sb")
        proj_ps, x1_ready, xn2_ready, xn2T_ps, xn2T_sb = (
            sem("proj_ps"), sem("x1_ready"), sem("xn2_ready"), sem("xn2T_ps"), sem("xn2T_sb"))
        tq_ps, tq_sb, c2_sb = sem("tq_ps"), sem("tq_sb"), sem("c2_sb")
        sc2_ps, sm_ready, nb2_ready, prob2_ready = (
            sem("sc2_ps"), sem("sm_ready"), sem("nb2_ready"), sem("prob2_ready"))
        v_ps, v_sb, prob2T_ps, prob2T_sb = sem("v_ps"), sem("v_sb"), sem("prob2T_ps"), sem("prob2T_sb")
        z_ps, x2_ready, xn3_ready, xn3T_ps, xn3T_sb = (
            sem("z_ps"), sem("x2_ready"), sem("xn3_ready"), sem("xn3T_ps"), sem("xn3T_sb"))
        xh_ready, xl_ready = sem("xh_ready"), sem("xl_ready")
        route_ps, rz_ready, sig_ready, gap_ready, tanh_done = (
            sem("route_ps"), sem("rz_ready"), sem("sig_ready"), sem("gap_ready"), sem("tanh_done"))
        chosen_ready, rank_ps, expert_ready, rows_of_ready = (
            sem("chosen_ready"), sem("rank_ps"), sem("expert_ready"), sem("rows_of_ready"))
        slots_zeroed, notes_blank, scattered, notes_ready, noted = (
            sem("slots_zeroed"), sem("notes_blank"), sem("scattered"), sem("notes_ready"), sem("noted"))
        whi_ready, wlo_ready = sem("whi_ready"), sem("wlo_ready")
        hidden_ps, gelu_done, hhi_ready, hlo_ready = (
            sem("hidden_ps"), sem("gelu_done"), sem("hhi_ready"), sem("hlo_ready"))
        down_ps, shared_read = sem("down_ps"), sem("shared_read")
        xrowT_ps, xrowT_sb, slot_hidden_ps, slot_gelu = (
            sem("xrowT_ps"), sem("xrowT_sb"), sem("slot_hidden_ps"), sem("slot_gelu"))
        slot_down_ps, result_row_ready, y_rows_ready, y_rows_out = (
            sem("slot_down_ps"), sem("result_row_ready"), sem("y_rows_ready"), sem("y_rows_out"))
        slot_hhi_ready, slot_hlo_ready, dhi_ready, dlo_ready = (
            sem("slot_hhi_ready"), sem("slot_hlo_ready"), sem("dhi_ready"), sem("dlo_ready"))
        picked_in = [sem(f"picked{t}_in") for t in range(T)]
        y_ready, y_out = sem("y_ready"), sem("y_out")

        H_BANKS = (0, 1, 4)
        SHARED_BANK = 2
        SLOT_OUT_BANKS, SLOT_X_BANK = (4, 6), 5
        ROUTE_BANK, RANK_BANK = 6, 7
        ORDER = plan()
        NORMS = {item: 2 + n for n, item in enumerate(item for item in ORDER if item[0] in ("proj", "z"))}

        def unit_at(n):
            return (n // J) % SHARED, n % J, n // (SHARED * J)

        block = whole.enter_context(nc.Block())

        @block.sync
        def _(sp):
            sp.dma_start(squares[:, 0:2], squares_d[:, 0:2]).then_inc(query_squares_in, 16)
            sp.dma_start(xs[:, :, :], x_d.rearrange("(t p) d -> p t d", p=P)).then_inc(x_in, 16)
            sp.dma_start(cols[:, :, :], cols_d.rearrange("(c p) n -> p c n", p=P)).then_inc(cols_in, 16)

            def load_ctxT(t):
                if t >= 2:
                    sp.wait_ge(scores_ps, SCH * (t - 1))
                for half, s in enumerate((slice(0, 2 * BANK), slice(2 * BANK, KV))):
                    sp.dma_start(ctxT[t % 2][:, :, :, s],
                                 ctxT_d[2 * t:2 * t + 2, :, s].rearrange("b (c p) k -> p b c k", p=P)
                                 ).then_inc(ctxT_in[t % 2][half], 16)

            def load_ctx(t):
                if t >= 2:
                    sp.wait_ge(pv_ps, t - 1)
                for b in range(2):
                    sp.dma_start(ctx[t % 2][:, b, 0:KT - 1, :],
                                 ctx_d[2 * t + b, 0:(KT - 1) * P].rearrange("(k p) d -> p k d", p=P)
                                 ).then_inc(ctx_in[t % 2], 16)
                    sp.dma_start(ctx[t % 2][0:KREM, b, KT - 1, :],
                                 ctx_d[2 * t + b, (KT - 1) * P:KV]).then_inc(ctx_in[t % 2], 16)

            load_ctxT(0)
            sp.dma_start(squares[:, 2:7], squares_d[:, 2:7]).then_inc(squares_in, 16)
            sp.dma_start(rows[:, :], rows_d.partition_broadcast(P)).then_inc(rows_in, 16)
            load_ctx(0)
            load_ctxT(1)
            for t in range(1, T - 1):
                load_ctxT(t + 1)
                load_ctx(t)
            load_ctx(T - 1)
            sp.dma_start(raw[0][:, :, :], experts_d[0]).then_inc(raw_in[0], 16)
            sp.wait_ge(pv_ps, T - 1)
            sp.wait_ge(scores_ps, SCH * (T - 1))
            sp.dma_start(raw[1][:, :, :], experts_d[1]).then_inc(raw_in[1], 16)
            sp.wait_ge(consts, 7)
            sp.dma_start(slot_x_d.rearrange("(s p) d -> p s d", p=P),
                         zeros[:, :].unsqueeze(1).to_broadcast([P, SLOTS, D])).then_inc(slots_zeroed, 16)
            sp.dma_start(notes_d.rearrange("(s p) n -> p s n", p=P), blank_notes[:, :, :]).then_inc(notes_blank, 16)

            def load(b, expert):
                sp.dma_start(ring[b][:, :, :], experts_d[bass.ds(expert + SHARED, 1)].rearrange("e p j w -> p (e j) w")
                             ).then_inc(ring_in[b], 16)

            sp.wait_ge(pv_ps, T)
            load(2, 2)
            load(3, 3)
            sp.wait_ge(wlo_ready, J)
            load(0, 0)
            sp.wait_ge(wlo_ready, 2 * J)
            load(1, 1)
            slots_x = slot_x_d.rearrange("(s p) d -> p s d", p=P)

            def load_rows(b, slot):
                sp.dma_start(xrow[:, b, :], slots_x[:, bass.ds(slot, 1), :].rearrange("p s d -> p (s d)")
                             ).then_inc(xrow_in[b], 16)

            sp.wait_ge(scattered, 16 * TOP * T)
            sp.wait_ge(down_ps, UNITS - J)
            for b in range(RING):
                load_rows(b, b)
            sp.wait_ge(noted, 16 * TOP * T)
            sp.dma_start(slot_notes[:, :, :], notes_d.rearrange("(s p) n -> p s n", p=P)).then_inc(notes_in, 16)
            sp.wait_ge(expert_ready, 1)

            def feed(b, slot):
                expert = sp.value_load(expert_of[0:1, bass.ds(slot, 1)], min_val=0, max_val=ROUTED - 1)
                sp.wait_ge(xrowT_ps, slot - RING + 1)
                load_rows(b, slot)
                sp.wait_ge(slot_hidden_ps, 2 * (slot - RING) + 2)
                sp.wait_ge(dlo_ready, 2 * (slot - RING) + 2)
                load(b, expert)

            with sp.Fori(1, SLOTS // RING) as turn:
                for b in range(RING):
                    feed(b, turn * RING + b)
            for b in range(SLOTS % RING):
                feed(b, SLOTS - SLOTS % RING + b)
            sp.wait_ge(y_rows_out, 16 * SLOTS)
            results = results_d[0:TOP * N].rearrange("(k t p) d -> p k t d", k=TOP, p=P)
            for t in range(T):
                sp.dma_start(picked[:, :, t, :], results[:, :, t, :]).then_inc(picked_in[t], 16)
            for t in range(T):
                sp.wait_ge(y_ready, t + 1)
                sp.dma_start(out_d[t * P:(t + 1) * P, :], xs[:, t, :]).then_inc(y_out, 16)
            sp.wait_ge(y_out, 16 * T)

        @block.gpsimd
        def _(pool):
            own = [0]

            def link(ins):
                own[0] += 1
                ins.then_inc(pool_own, 1)
                pool.wait_ge(pool_own, own[0])

            pool.memset(neghalf[:, :], -0.5).then_inc(consts, 1)
            link(pool.memset(ident[:, :], 0.0))
            pool.affine_select(out=ident[:, :], in_=ident[:, :], compare_op=ALU.not_equal, fill=1.0, base=0,
                               pattern=[[-1, P]], channel_multiplier=1).then_inc(consts, 1)
            pool.memset(ones[:, :], 1.0).then_inc(consts, 1)
            link(pool.memset(mask[:, :], 0.0))
            link(pool.affine_select(out=mask[:, :], in_=mask[:, :], compare_op=ALU.is_ge, fill=MASKED, base=0,
                                    pattern=[[-1, P]], channel_multiplier=1))
            pool.memset(mask[SQ:P, 0:SQ], MASKED).then_inc(consts, 1)
            pool.wait_ge(consts, 4)
            link(pool.memset(tri[:, :], 1.0))
            pool.affine_select(out=tri[:, :], in_=tri[:, :], compare_op=ALU.is_ge, fill=0.0, base=-1,
                               pattern=[[1, P]], channel_multiplier=-1).then_inc(consts, 1)
            pool.memset(zeros[:, :], 0.0).then_inc(consts, 1)
            pool.wait_ge(consts, 6)
            link(pool.iota(iota128[:, :], pattern=[[P, ROUTED]], base=0, channel_multiplier=0,
                           allow_small_or_imprecise_dtypes=True))
            link(pool.iota(over_no[:, :, :], pattern=[[1, OVER], [0, ROUTED]], base=0, channel_multiplier=0,
                           allow_small_or_imprecise_dtypes=True))
            link(pool.iota(expert_f[:, :], pattern=[[1, SLOTS]], base=0, channel_multiplier=0,
                           allow_small_or_imprecise_dtypes=True))
            link(pool.memset(blank_notes[:, :, :], 0.0))
            link(pool.iota(blank_notes[:, :, 0], pattern=[[P, SLOTS]], base=TOP * N, channel_multiplier=1,
                           allow_small_or_imprecise_dtypes=True))
            for k in range(TOP):
                link(pool.iota(notes[:, k, :, 0], pattern=[[P, T]], base=k * N, channel_multiplier=1,
                               allow_small_or_imprecise_dtypes=True))
            link(pool.memset(before[:, 0, :], 0.0))
            link(pool.memset(ones8[:, :], 1.0))
            pool.iota(iota8[:, :, :], pattern=[[0, T], [1, ROUTED]], base=0, channel_multiplier=0,
                      allow_small_or_imprecise_dtypes=True).then_inc(consts, 1)
            pool.wait_ge(consts, 7)
            pool.wait_ge(var_ready, 1)
            pool.tensor_tensor(rstd[:, :], veps[:, :], neghalf[:, :], ALU.pow).then_inc(rstd_ready, 1)
            for what, *args in ORDER:
                if what in ("proj", "z"):
                    t, = args
                    pool.wait_ge(var_ready, NORMS[what, t])
                    pool.tensor_tensor(rstd[:, t:t + 1], veps[:, t:t + 1], neghalf[:, t:t + 1], ALU.pow
                                       ).then_inc(rstd_ready, 1)
            pool.wait_ge(slots_zeroed, 16)
            pool.wait_ge(rows_of_ready, 1)
            for k in range(TOP):
                for t in range(T):
                    pool.indirect_dma_start(out=slot_x_d,
                                            out_offset=bass.IndirectOffsetOnAxis(ap=rows_of[:, k, t:t + 1], axis=0),
                                            in_=xn[:, t, :], in_offset=None).then_inc(scattered, 16)
            pool.wait_ge(notes_blank, 16)
            pool.wait_ge(notes_ready, 1)
            for k in range(TOP):
                for t in range(T):
                    pool.indirect_dma_start(out=notes_d,
                                            out_offset=bass.IndirectOffsetOnAxis(ap=rows_of[:, k, t:t + 1], axis=0),
                                            in_=notes[:, k, t, :], in_offset=None).then_inc(noted, 16)
            pool.wait_ge(notes_in, 16)
            pool.tensor_copy(result_row[:, :], slot_notes[:, :, 0]).then_inc(result_row_ready, 1)
            pool.wait_ge(result_row_ready, 1)
            for slot in range(SLOTS):
                pool.wait_ge(y_rows_ready, slot + 3)
                pool.indirect_dma_start(out=results_d,
                                        out_offset=bass.IndirectOffsetOnAxis(ap=result_row[:, slot:slot + 1], axis=0),
                                        in_=y_rows[:, slot, :], in_offset=None).then_inc(y_rows_out, 16)

        @block.tensor
        def _(pe):
            def mm(out, lhsT, rhs, first, last):
                return pe.matmul(out, lhsT, rhs, start=first, stop=last)

            def fold(b, left, right):
                for m in range(C):
                    for k in range(C):
                        ins = mm(bank(b, m * D, D), squares[:, left, k, m * P:(m + 1) * P],
                                 squares[:, right, k, 0:D], k == 0, k == C - 1)
                ins.then_inc(fold_ps, 1)

            def fold_vec(b, at, left, col):
                for m in range(C):
                    for k in range(C):
                        ins = mm(bank(b, at + m, 1), squares[:, left, k, m * P:(m + 1) * P],
                                 cols[:, k, col:col + 1], k == 0, k == C - 1)
                return ins

            def fold_row(b, spread, right):
                for k in range(C):
                    ins = mm(bank(b, 0, D + 1), bcast[:, spread, k, :], squares[:, right, k, :], k == 0, k == C - 1)
                return ins

            pe.wait_ge(query_squares_in, 16)
            fold(0, XWQT, XWKT)
            pe.wait_ge(cols_in, 16)
            fold_vec(1, D + 1, XWKT, XBQ)
            pe.wait_ge(bcast_ready, 1)
            fold_row(1, 0, XWQT).then_inc(fold_ps, 1)
            pe.wait_ge(consts, 7)
            pe.wait_ge(xn1_ready, T)
            for t in range(T):
                for c in range(C):
                    ins = pe.transpose(bank(PT + t // 2, (t % 2) * D + c * P, P),
                                       xn[:, t, c * P:(c + 1) * P], ident[:, :])
                if t % 2 == 1:
                    ins.then_inc(xT_ps, 1)
            pe.wait_ge(fold_act, 1)
            for t in range(T):
                pe.wait_ge(xT_sb, t // 2 + 1)
                tok = slice(t * P, (t + 1) * P)
                for m in range(C):
                    for k in range(C):
                        ins = mm(bank(PO + t // 2, (t % 2) * D + m * P, P), aq[:, k, m * P:(m + 1) * P],
                                 xT[:, k, tok], k == 0, k == C - 1)
                if t % 2 == 1:
                    ins.then_inc(q_ps, 1)

            def scores(t, ch):
                if t % 2 == 0 and ch == 0:
                    pe.wait_ge(q_sb, t // 2 + 1)
                if t == 0 and ch == 0:
                    pe.wait_ge(fold_act, 1)
                    pe.wait_ge(fold_dve, 1)
                if ch % 2 == 0:
                    pe.wait_ge(ctxT_in[t % 2][ch // 2], 16 * (t // 2 + 1))
                if t >= 1:
                    pe.wait_ge(exp_done, SCH * (t - 1) + ch + 1)
                s = scols(ch)
                for c in range(C):
                    for b in range(2):
                        ins = mm(psum[b * SQ:(b + 1) * SQ, s], qT[:, c, t * P + b * SQ:t * P + (b + 1) * SQ],
                                 ctxT[t % 2][:, b, c, s], c == 0, c == C - 1)
                ins.then_inc(scores_ps, 1)

            def transpose_probs(t, g):
                if g == 0:
                    pe.wait_ge(exp_done, SCH * (t + 1))
                if g == 0 and t >= 1:
                    pe.wait_ge(probT_act, 3 * t - 1)
                elif g == 1 and t >= 1:
                    pe.wait_ge(probT_act, 3 * t)
                elif g == 2:
                    pe.wait_ge(probT_act, 3 * t + 1)
                elif g == 3:
                    pe.wait_ge(probT_dve, t + 1)
                for k in range(4 * g, min(4 * g + 4, KT)):
                    r = P if k < KT - 1 else KREM
                    ins = pe.transpose(bank(PT + g % 2, (k % 4) * P, P)[0:r, :],
                                       prob[:, k * P:k * P + r], ident[:, :])
                ins.then_inc(probT_ps, 1)

            def weigh(t, k0, k1):
                if k0 == 0:
                    pe.wait_ge(ctx_in[t % 2], 64 * (t // 2 + 1))
                    if t == 0:
                        pe.wait_ge(fold_dve, 4)
                    pe.wait_ge(probT_act, 3 * (t + 1))
                    pe.wait_ge(probT_dve, t + 1)
                    if t >= 1:
                        pe.wait_ge(mix_ready, t)
                for k in range(k0, k1):
                    r = P if k < KT - 1 else KREM
                    for b in range(2):
                        ins = mm(bank(PO, 0, D)[b * SQ:(b + 1) * SQ, :], probT[0:r, k, b * SQ:(b + 1) * SQ],
                                 ctx[t % 2][0:r, b, k, :], k == 0, k == KT - 1)
                if k1 == KT:
                    ins.then_inc(pv_ps, 1)

            def chain_mixT(t):
                pe.wait_ge(mix_ready, t + 1)
                if 1 <= t < T - 1:
                    pe.wait_ge(xn3T_sb, t)
                for c in range(C):
                    ins = pe.transpose(bank(chain_bank(t), c * P, P), mix[:, c * P:(c + 1) * P], ident[:, :])
                ins.then_inc(mixT_ps, 1)

            def chain_proj(t):
                pe.wait_ge(mixT_sb, t + 1)
                if t == 0:
                    pe.wait_ge(fold_act, 2)
                for c in range(C):
                    ins = mm(bank(chain_bank(t), 0, D), mixT[:, c, :], wvo[:, c, :], c == 0, c == C - 1)
                ins.then_inc(proj_ps, 1)

            def chain_xn2T(t):
                pe.wait_ge(xn2_ready, t + 1)
                for c in range(C):
                    ins = pe.transpose(bank(chain_bank(t), c * P, P), xn[:, t, c * P:(c + 1) * P], ident[:, :])
                ins.then_inc(xn2T_ps, 1)

            def chain_tq(t):
                pe.wait_ge(xn2T_sb, t + 1)
                if t == 0:
                    pe.wait_ge(fold_act, 3)
                for m in range(C):
                    for k in range(C):
                        ins = mm(bank(chain_bank(t), m * P, P), a2[:, k, m * P:(m + 1) * P], xn2T[:, k, :],
                           k == 0, k == C - 1)
                ins.then_inc(tq_ps, 1)

            def chain_scores(t):
                pe.wait_ge(tq_sb, C * (t + 1))
                for c in range(C):
                    ins = mm(bank(chain_bank(t), 0, P), tq[:, c, :], xn2T[:, c, :], c == 0, c == C - 1)
                ins.then_inc(sc2_ps, 1)

            def chain_v(t):
                pe.wait_ge(sm_ready, t + 1)
                for c in range(C):
                    ins = mm(bank(chain_bank(t), 0, D), xn2T[:, c, :], squares[:, AWVT, c, 0:D], c == 0, c == C - 1)
                ins.then_inc(v_ps, 1)

            def chain_prob2T(t):
                pe.wait_ge(prob2_ready, t + 1)
                pe.wait_ge(v_sb, t + 1)
                pe.transpose(bank(chain_bank(t), 0, P), prob2[:, :], ident[:, :]).then_inc(prob2T_ps, 1)

            def chain_z(t):
                pe.wait_ge(prob2T_sb, t + 1)
                mm(bank(chain_bank(t), 0, D), prob2T[:, :], v2[:, :], True, True).then_inc(z_ps, 1)

            def chain_xn3T(t):
                pe.wait_ge(xn3_ready, t + 1)
                for c in range(C):
                    ins = pe.transpose(bank(chain_bank(t), c * P, P), xn[:, t, c * P:(c + 1) * P], ident[:, :])
                ins.then_inc(xn3T_ps, 1)

            for ch in range(SCH):
                scores(0, ch)
            pe.wait_ge(squares_in, 16)
            for m in range(C):
                for k in range(C):
                    ins = mm(bank(PT, m * D, D), squares[:, XWVT, k, m * P:(m + 1) * P],
                             squares[:, XWO, k, 0:D], k == 0, k == C - 1)
            ins.then_inc(fold_ps, 1)
            for m in range(C):
                for k in range(C):
                    ins = mm(bank(PT + 1, m * D, D), squares[:, AWQ, k, m * P:(m + 1) * P],
                             squares[:, AWK, k, 0:D], k == 0, k == C - 1)
            ins.then_inc(fold_ps, 1)
            pe.wait_ge(q_sb, 2)
            for k in range(C):
                mm(bank(PO, 0, D), bcast[:, 1, k, :], squares[:, XWO, k, 0:D], k == 0, k == C - 1)
            fold_vec(PO, D, AWK, ABQ)
            pe.wait_ge(bcast_ready, 3)
            fold_row(CHAIN, 2, AWQ).then_inc(fold_ps, 1)
            pe.wait_ge(fold_act, 3)

            def route(t):
                pe.wait_ge(xn3T_sb, t + 1)
                for c in range(C):
                    ins = mm(bank(ROUTE_BANK, t * ROUTED, ROUTED), xT[:, c, t * P:(t + 1) * P],
                             cols[:, c, CENT:CENT + ROUTED], c == 0, c == C - 1)
                ins.then_inc(route_ps, 1)

            def ranks():
                pe.wait_ge(chosen_ready, 1)
                mm(bank(RANK_BANK, 0, T * ROUTED), tri[:, :], chosen[:, :, :].rearrange("p t e -> p (t e)"),
                   True, False)
                mm(bank(RANK_BANK, 0, T * ROUTED), ones[:, :], before[:, :, :].rearrange("p t e -> p (t e)"),
                   False, True)
                mm(bank(RANK_BANK, T * ROUTED, ROUTED), ones[:, :], total[:, :], True, True).then_inc(rank_ps, 1)

            def hidden(n, tok):
                w, j, _ = unit_at(n)
                h = bank(H_BANKS[n % LEAD], 0, tok.stop - tok.start)
                parts = ((whi, xh), (whi, xl), (wlo, xh))
                for c in range(C):
                    for p, (wp, xp) in enumerate(parts):
                        ins = mm(h, wp[w][:, j, c * P:(c + 1) * P], xp[:, c, tok],
                                 c == 0 and p == 0, c == C - 1 and p == len(parts) - 1)
                ins.then_inc(hidden_ps, 1)

            def unit_down(n):
                e, j, half = unit_at(n)
                for p, (hp, wp) in enumerate(((hhi, whi), (hhi, wlo), (hlo, whi))):
                    if hp is hhi:
                        pe.wait_ge(hhi_ready, n + 1)
                    else:
                        pe.wait_ge(hlo_ready, n + 1)
                    for tile in range(2):
                        first = (e, j, p, tile) == (0, 0, 0, 0)
                        last = (e, j, p) == (SHARED - 1, J - 1, 2)
                        ins = pe.matmul(bank(SHARED_BANK + half, tile * D, D),
                                        hp[:, n % LEAD, tile * P:(tile + 1) * P], wp[e][:, j, C * P:STEP_W],
                                        start=first, stop=last, skip_group_check=True)
                ins.then_inc(down_ps, 1)

            def unit_hidden(n):
                if n >= LEAD:
                    pe.wait_ge(gelu_done, n - LEAD + 1)
                e, j, half = unit_at(n)
                pe.wait_ge(xl_ready, 2 * (half + 1))
                pe.wait_ge(wlo_ready, J * e + j + 1)
                hidden(n, slice(half * HALF, (half + 1) * HALF))

            def unit(n):
                unit_down(n)
                if n + LEAD < UNITS:
                    unit_hidden(n + LEAD)

            def slot_rows(b, n):
                pe.wait_ge(xrow_in[b], 16 * n)
                for c in range(C):
                    ins = pe.transpose(bank(SLOT_X_BANK, c * P, P), xrow[:, b, c * P:(c + 1) * P], ident[:, :])
                ins.then_inc(xrowT_ps, 1)

            mine = {"T": transpose_probs, "S": scores, "W": weigh, "mixT": chain_mixT, "proj": chain_proj,
                    "xn2T": chain_xn2T, "tq": chain_tq, "sc": chain_scores, "v": chain_v,
                    "probT": chain_prob2T, "z": chain_z, "xn3T": chain_xn3T, "lead": unit_hidden,
                    "unit": unit, "route": route, "rank": ranks, "slot_rows": lambda: slot_rows(0, 1)}
            for what, *args in ORDER:
                if what in mine:
                    mine[what](*args)

            def slot_hidden(b, half):
                for j in range(4 * half, 4 * half + 4):
                    for c in range(C):
                        ins = mm(bank(H_BANKS[half], (j % 4) * P, P), ring[b][:, j, c * P:(c + 1) * P],
                                 xrowT[:, c, :], c == 0, c == C - 1)
                ins.then_inc(slot_hidden_ps, 1)

            def slot_start(slot, b, n):
                pe.wait_ge(ring_in[b], 16 * n)
                pe.wait_ge(xrowT_sb, slot + 1)
                slot_hidden(b, 0)

            def slot_down(slot, b, half):
                if half == 0:
                    pe.wait_ge(y_rows_ready, slot + 1)
                pe.wait_ge(slot_hlo_ready, 2 * slot + half + 1)
                pe.wait_ge(dlo_ready, 2 * slot + half + 1)
                for j in range(4 * half, 4 * half + 4):
                    h = slice((j % 4) * P, (j % 4 + 1) * P)
                    for p, (hp, wp) in enumerate(((slot_hhi, dhi), (slot_hhi, dlo), (slot_hlo, dhi))):
                        ins = mm(bank(SLOT_OUT_BANKS[b % 2], 0, D), hp[:, half, h], wp[b % 2][:, j, :],
                                 (j, p) == (0, 0), (j, p) == (J - 1, 2))
                if half == 1:
                    ins.then_inc(slot_down_ps, 1)

            def slot_step(slot, b, n, last=False):
                slot_hidden(b, 1)
                after, n_after = (b + 1) % RING, n + (b + 1) // RING
                if not last:
                    slot_rows(after, n_after)
                slot_down(slot, b, 0)
                if not last:
                    slot_start(slot + 1, after, n_after)
                slot_down(slot, b, 1)

            pe.wait_ge(gelu_done, UNITS)
            slot_start(0, 0, 1)
            with pe.Fori(0, SLOTS // RING) as turn:
                for b in range(RING):
                    slot_step(turn * RING + b, b, turn + 1)
            for b in range(SLOTS % RING):
                slot = SLOTS - SLOTS % RING + b
                slot_step(slot, b, SLOTS // RING + 1, last=slot == SLOTS - 1)

        @block.scalar
        def _(act):
            act.wait_ge(fold_ps, 1)
            act.activation(aq[:, :, :].rearrange("p c d -> p (c d)"), bank(0), ACT.Copy, scale=SCALE
                           ).then_inc(fold_act, 1)
            for h in range(2):
                act.wait_ge(xT_ps, h + 1)
                act.activation(xT[:, :, 2 * h * P:2 * (h + 1) * P].rearrange("p c (t n) -> p t c n", t=2),
                               bank(PT + h).rearrange("p (t c n) -> p t c n", t=2, c=C), ACT.Copy
                               ).then_inc(xT_sb, 1)
            act.wait_ge(fold_dve, 1)
            for h in range(2):
                act.wait_ge(q_ps, h + 1)
                for c in range(C):
                    ins = act.activation(qT[:, c, 2 * h * P:2 * (h + 1) * P].rearrange("p (t n) -> p t n", t=2),
                                         bank(PO + h).rearrange("p (t c n) -> p t c n", t=2, c=C)[:, :, c, :],
                                         ACT.Identity, bias=vecs[:, c:c + 1])
                ins.then_inc(q_sb, 1)
            def exps(t, ch):
                act.wait_ge(nb_ready, t + 1)
                s = scols(ch)
                act.activation(prob[:, s], psum[:, s], ACT.Exp, bias=nb[:, :], accum_out=lsum[:, t % 2, ch:ch + 1]
                               ).then_inc(exp_done, 1)

            def probT_copy(t, g):
                if g == 1:
                    return
                act.wait_ge(probT_ps, TG * t + g + 1)
                if g == TG - 1:
                    ins = act.activation(probT[0:KREM, KT - 1, :], bank(PT + g % 2, 0, P)[0:KREM, :], ACT.Copy)
                else:
                    ins = act.activation(probT[:, 4 * g:4 * g + 4, :].rearrange("p k n -> p (k n)"),
                                         bank(PT + g % 2), ACT.Copy)
                ins.then_inc(probT_act, 1)

            def xn2T_copy(t):
                act.wait_ge(xn2T_ps, t + 1)
                act.activation(xn2T[:, :, :].rearrange("p c n -> p (c n)"), bank(chain_bank(t), 0, D), ACT.Copy
                               ).then_inc(xn2T_sb, 1)

            def tq_copy(t):
                act.wait_ge(tq_ps, t + 1)
                for c in range(C):
                    act.activation(tq[:, c, :], bank(chain_bank(t), c * P, P), ACT.Identity,
                                   bias=vecs[:, C + c:C + c + 1]).then_inc(tq_sb, 1)

            def exp2(t):
                act.wait_ge(nb2_ready, t + 1)
                act.activation(prob2[:, :], sm[:, :], ACT.Exp, bias=nb2[:, :], accum_out=lsum2[:, :]
                               ).then_inc(prob2_ready, 1)

            def prob2T_copy(t):
                act.wait_ge(prob2T_ps, t + 1)
                act.activation(prob2T[:, :], bank(chain_bank(t), 0, P), ACT.Copy).then_inc(prob2T_sb, 1)

            def xn3T_copy(t):
                tok = slice(t * P, (t + 1) * P)
                act.wait_ge(xn3T_ps, t + 1)
                act.activation(xT[:, :, tok], bank(chain_bank(t), 0, D).rearrange("p (c n) -> p c n", c=C), ACT.Copy
                               ).then_inc(xn3T_sb, 1)
                act.wait_ge(xn3T_sb, t + 1)
                act.activation(xh[:, :, tok], xT[:, :, tok], ACT.Copy).then_inc(xh_ready, 1)

            def split_high(j, w):
                act.activation(whi[w][:, j, :], raw[w][:, j, :], ACT.Copy).then_inc(whi_ready, 1)

            def split(q):
                e, j = q // J, q % J
                if j == 0:
                    act.wait_ge(raw_in[e % 2], 16 * (e // 2 + 1))
                if q == 0:
                    act.wait_ge(pv_ps, T - 1)
                if q == J:
                    act.wait_ge(pv_ps, T)
                split_high(j, e % 2)

            def stage(n):
                act.wait_ge(hidden_ps, n + 1)
                if n >= LEAD:
                    act.wait_ge(hlo_ready, n - LEAD + 1)
                act.activation(hraw[:, n % LEAD, :], bank(H_BANKS[n % LEAD], 0, HALF), ACT.Gelu).then_inc(gelu_done, 1)
                act.wait_ge(gelu_done, n + 1)
                if n >= LEAD:
                    act.wait_ge(down_ps, n - LEAD + 1)
                act.activation(hhi[:, n % LEAD, :], hraw[:, n % LEAD, :], ACT.Copy).then_inc(hhi_ready, 1)

            def unit(n):
                if n + LEAD < UNITS:
                    stage(n + LEAD)

            def route():
                act.wait_ge(rz_ready, 2)
                act.activation(sg[:, :, :, :].rearrange("p a t e -> p (a t e)"),
                               rz[:, :, :, :].rearrange("p a t e -> p (a t e)"), ACT.Exp, scale=-1.0
                               ).then_inc(sig_ready, 1)

            def gates():
                act.wait_ge(gap_ready, 1)
                act.activation(gap[:, :], gap[:, :], ACT.Tanh, scale=0.5).then_inc(tanh_done, 1)

            def split_down(b, half):
                steps = slice(4 * half, 4 * half + 4)
                act.activation(dhi[b % 2][:, steps, :], ring[b][:, steps, C * P:STEP_W], ACT.Copy
                               ).then_inc(dhi_ready, 1)

            def first_split_down(half):
                act.wait_ge(ring_in[0], 16)
                split_down(0, half)

            for ch in range(SCH):
                exps(0, ch)
            act.wait_ge(fold_ps, 3)
            act.activation(wvo[:, :, :].rearrange("p c d -> p (c d)"), bank(PT), ACT.Copy).then_inc(fold_act, 1)
            act.wait_ge(fold_ps, 4)
            act.activation(a2[:, :, :].rearrange("p c d -> p (c d)"), bank(PT + 1), ACT.Copy, scale=SCALE
                           ).then_inc(fold_act, 1)
            mine = {"T": probT_copy, "exp": exps, "xn2T": xn2T_copy, "tq": tq_copy, "exp2": exp2,
                    "probT": prob2T_copy, "xn3T": xn3T_copy, "split": split, "unit": unit,
                    "lead": stage, "sigmoid": route, "gates": gates,
                    "slot_down": first_split_down}
            for what, *args in ORDER:
                if what in mine:
                    mine[what](*args)

            def slot_features(slot, half):
                act.wait_ge(slot_hidden_ps, 2 * slot + half + 1)
                act.activation(slot_h[:, half, :], bank(H_BANKS[half]), ACT.Gelu).then_inc(slot_gelu, 1)
                act.wait_ge(slot_gelu, 2 * slot + half + 1)
                act.activation(slot_hhi[:, half, :], slot_h[:, half, :], ACT.Copy).then_inc(slot_hhi_ready, 1)

            def slot_step(slot, b, n, last=False):
                slot_features(slot, 1)
                if not last:
                    after, n_after = (b + 1) % RING, n + (b + 1) // RING
                    act.wait_ge(ring_in[after], 16 * n_after)
                    split_down(after, 0)
                    slot_features(slot + 1, 0)
                    split_down(after, 1)

            slot_features(0, 0)
            with act.Fori(0, SLOTS // RING) as turn:
                for b in range(RING):
                    slot_step(turn * RING + b, b, turn + 1)
            for b in range(SLOTS % RING):
                slot = SLOTS - SLOTS % RING + b
                slot_step(slot, b, SLOTS // RING + 1, last=slot == SLOTS - 1)

        @block.vector
        def _(dve):
            own = [0]

            def link(ins):
                own[0] += 1
                ins.then_inc(dve_own, 1)
                dve.wait_ge(dve_own, own[0])

            def stats_of(t):
                link(dve.bn_stats(stats[:, t, :], xs[:, t, :]))
                link(dve.bn_aggr(mv[:, t, :], stats[:, t, :]))
                dve.tensor_scalar(veps[:, t:t + 1], mv[:, t, 1:2], EPS, None, ALU.add).then_inc(var_ready, 1)

            def norm(t, ready):
                dve.wait_ge(rstd_ready, ready)
                return dve.tensor_scalar(xn[:, t, :], xs[:, t, :], mv[:, t, 0:1], rstd[:, t:t + 1],
                                         ALU.subtract, ALU.mult)

            def q_dot_bk(out, t, attention):
                return dve.tensor_tensor_reduce(product[:, :], xn[:, t, :], wrow[:, attention, 0:D], 1.0,
                                                wrow[:, attention, D:D + 1], ALU.mult, ALU.add, out)

            dve.wait_ge(x_in, 16)
            for t in range(T):
                ins = dve.bn_stats(stats[:, t, :], xs[:, t, :])
            link(ins)
            for t in range(T):
                ins = dve.bn_aggr(mv[:, t, :], stats[:, t, :])
            link(ins)
            dve.tensor_scalar(veps[:, :], mv[:, :, 1], EPS, None, ALU.add).then_inc(var_ready, 1)
            dve.wait_ge(consts, 7)
            dve.wait_ge(cols_in, 16)
            for n, col in enumerate((XBK, XBV, ABK)):
                for c in range(C):
                    ins = dve.tensor_scalar(bcast[:, n, c, :], ones[:, :], cols[:, c, col:col + 1], None, ALU.mult)
                ins.then_inc(bcast_ready, 1)
            dve.wait_ge(rstd_ready, 1)
            for t in range(T):
                dve.tensor_scalar(xn[:, t, :], xs[:, t, :], mv[:, t, 0:1], rstd[:, t:t + 1],
                                  ALU.subtract, ALU.mult).then_inc(xn1_ready, 1)
            dve.wait_ge(fold_ps, 2)
            dve.tensor_scalar(wrow[:, 0, :], bank(1, 0, D + 1), SCALE, None, ALU.mult)
            dve.tensor_scalar(vecs[:, 0:C], bank(1, D + 1, C), SCALE, None, ALU.mult).then_inc(fold_dve, 1)
            dve.wait_ge(fold_dve, 1)
            for t in range(T):
                link(q_dot_bk(cq[:, t:t + 1], t, 0))

            def max_chunk(t, ch):
                dve.wait_ge(scores_ps, SCH * t + ch + 1)
                ins = dve.tensor_reduce(cmax[:, ch:ch + 1], psum[:, scols(ch)], AX_X, ALU.max)
                if ch == SCH - 1:
                    link(ins)
                    link(dve.tensor_reduce(small[:, 0:1], cmax[:, :], AX_X, ALU.max))
                    link(dve.tensor_tensor(small[:, 1:2], small[:, 0:1], cq[:, t:t + 1], ALU.add))
                    if t >= 1:
                        dve.wait_ge(exp_done, SCH * t)
                    dve.tensor_tensor(nb[:, :], cq[:, t:t + 1], small[:, 1:2], ALU.subtract).then_inc(nb_ready, 1)

            for ch in range(SCH):
                max_chunk(0, ch)
            dve.wait_ge(fold_ps, 5)
            dve.wait_ge(rows_in, 16)
            dve.tensor_tensor(mix[:, :], bank(PO, 0, D), rows[:, 0:D], ALU.add).then_inc(fold_dve, 1)
            dve.tensor_scalar(vecs[:, C:2 * C], bank(PO, D, C), SCALE, None, ALU.mult).then_inc(fold_dve, 1)
            dve.tensor_scalar(wrow[:, 1, :], bank(CHAIN, 0, D + 1), SCALE, None, ALU.mult).then_inc(fold_dve, 1)

            def x_bias():
                dve.wait_ge(fold_dve, 2)
                for t in range(T):
                    ins = dve.tensor_tensor(xs[:, t, :], xs[:, t, :], mix[:, :], ALU.add)
                link(ins)

            def probT_copy(t, g):
                if g == 1:
                    dve.wait_ge(probT_ps, TG * t + g + 1)
                    dve.tensor_copy(probT[:, 4 * g:4 * g + 4, :].rearrange("p k n -> p (k n)"),
                                    bank(PT + g % 2)).then_inc(probT_dve, 1)

            def mix_scale(t):
                dve.wait_ge(exp_done, SCH * (t + 1))
                link(dve.tensor_reduce(small[:, 2:3], lsum[:, t % 2, :], AX_X, ALU.add))
                link(dve.reciprocal(linv[:, 0:1], small[:, 2:3]))
                dve.wait_ge(pv_ps, t + 1)
                dve.tensor_scalar(mix[:, :], bank(PO, 0, D), linv[:, 0:1], None, ALU.mult).then_inc(mix_ready, 1)

            def mixT_copy(t):
                dve.wait_ge(mixT_ps, t + 1)
                dve.tensor_copy(mixT[:, :, :].rearrange("p c n -> p (c n)"), bank(chain_bank(t), 0, D)
                                ).then_inc(mixT_sb, 1)

            def x1_add(t):
                dve.wait_ge(proj_ps, t + 1)
                dve.tensor_tensor(xs[:, t, :], bank(chain_bank(t), 0, D), xs[:, t, :], ALU.add).then_inc(x1_ready, 1)

            def norm2(t):
                norm(t, NORMS["proj", t]).then_inc(xn2_ready, 1)

            def c2_dot(t):
                dve.wait_ge(xn2_ready, t + 1)
                dve.wait_ge(fold_dve, 4)
                q_dot_bk(c2[:, :], t, 1).then_inc(c2_sb, 1)

            def softmax2(t):
                dve.wait_ge(sc2_ps, t + 1)
                dve.wait_ge(c2_sb, t + 1)
                dve.tensor_tensor(sm[:, :], bank(chain_bank(t), 0, P), mask[:, :], ALU.add).then_inc(sm_ready, 1)
                dve.wait_ge(sm_ready, t + 1)
                link(dve.tensor_reduce(small2[:, 0:1], sm[:, :], AX_X, ALU.max))
                link(dve.tensor_tensor(small2[:, 1:2], small2[:, 0:1], c2[:, :], ALU.add))
                dve.tensor_tensor(nb2[:, :], c2[:, :], small2[:, 1:2], ALU.subtract).then_inc(nb2_ready, 1)

            def v_copy(t):
                dve.wait_ge(v_ps, t + 1)
                dve.tensor_tensor(v2[:, :], bank(chain_bank(t), 0, D), rows[:, D:2 * D], ALU.add).then_inc(v_sb, 1)

            def x2_add(t):
                dve.wait_ge(prob2_ready, t + 1)
                link(dve.reciprocal(linv[:, 1:2], lsum2[:, :]))
                dve.wait_ge(z_ps, t + 1)
                dve.scalar_tensor_tensor(xs[:, t, :], bank(chain_bank(t), 0, D), linv[:, 1:2], xs[:, t, :],
                                         ALU.mult, ALU.add).then_inc(x2_ready, 1)
                dve.wait_ge(x2_ready, t + 1)
                stats_of(t)

            def norm3(t):
                norm(t, NORMS["z", t]).then_inc(xn3_ready, 1)
                dve.wait_ge(xn3_ready, t + 1)
                link(dve.tensor_tensor(xs[:, t, :], xs[:, t, :], xn[:, t, :], ALU.add))

            def split_x(t):
                tok = slice(t * P, (t + 1) * P)
                dve.wait_ge(xh_ready, t + 1)
                dve.tensor_tensor(xl[:, :, tok], xT[:, :, tok], xh[:, :, tok].bitcast(F32), ALU.subtract
                                  ).then_inc(xl_ready, 1)

            def x1_stats(t):
                x1_add(t)
                dve.wait_ge(x1_ready, t + 1)
                stats_of(t)

            def weigh(t, k0, k1):
                if k1 == KT:
                    mix_scale(t)

            def split_low(q, j, w):
                dve.wait_ge(whi_ready, q + 1)
                dve.tensor_tensor(wlo[w][:, j, :], raw[w][:, j, :], whi[w][:, j, :].bitcast(F32), ALU.subtract
                                  ).then_inc(wlo_ready, 1)

            def stage(n):
                dve.wait_ge(hhi_ready, n + 1)
                dve.tensor_tensor(hlo[:, n % LEAD, :], hraw[:, n % LEAD, :], hhi[:, n % LEAD, :].bitcast(F32),
                                  ALU.subtract).then_inc(hlo_ready, 1)

            def unit(n):
                if n + LEAD < UNITS:
                    stage(n + LEAD)

            def route():
                dve.wait_ge(route_ps, T)
                z = bank(ROUTE_BANK, 0, T * ROUTED).rearrange("p (t e) -> p t e", t=T)
                dve.tensor_copy(rz[:, 0, :, :], z).then_inc(rz_ready, 1)
                dve.tensor_tensor(rz[:, 1, :, :], z,
                                  rows[:, 2 * D:2 * D + ROUTED].unsqueeze(1).to_broadcast([P, T, ROUTED]),
                                  ALU.add).then_inc(rz_ready, 1)

            def top2():
                dve.wait_ge(sig_ready, 1)
                sgf = sg[:, :, :, :].rearrange("p a t e -> p (a t e)")
                link(dve.tensor_scalar(sgf, sgf, 1.0, None, ALU.add))
                link(dve.reciprocal(sgf, sgf))

            def indices():
                for t in range(T):
                    ins = dve.max(top8[:, t, :], sg[:, 1, t, :])
                link(ins)
                for t in range(T):
                    ins = dve.max_index(idx8[:, t, :], top8[:, t, :], sg[:, 1, t, :])
                link(ins)

            def mark():
                link(dve.tensor_copy(idxf[:, :, :], idx8[:, :, 0:TOP]))
                for k in range(TOP):
                    ins = dve.tensor_tensor(hot[:, k, :, :], iota8[:, :, :],
                                            idxf[:, :, k:k + 1].to_broadcast([P, T, ROUTED]), ALU.is_equal)
                link(ins)

            def choices():
                link(dve.tensor_tensor(chosen[:, :, :], hot[:, 0, :, :], hot[:, 1, :, :], ALU.add))
                for t in range(1, T):
                    link(dve.tensor_tensor(before[:, t, :], before[:, t - 1, :], chosen[:, t - 1, :], ALU.add))
                dve.tensor_tensor(total[:, :], before[:, T - 1, :], chosen[:, T - 1, :], ALU.add
                                  ).then_inc(chosen_ready, 1)

            def place():
                dve.wait_ge(rank_ps, 1)
                dve.tensor_copy(rank[:, :, :].rearrange("p t e -> p (t e)"), bank(RANK_BANK, 0, T * ROUTED))
                link(dve.tensor_copy(count[:, :], bank(RANK_BANK, T * ROUTED, ROUTED)))
                link(dve.tensor_scalar(over[:, 0, :], count[:, :], P + 0.5, None, ALU.is_gt))
                for most in (2 * P, 3 * P):
                    link(dve.scalar_tensor_tensor(over[:, 0, :], count[:, :], most + 0.5, over[:, 0, :],
                                                  ALU.is_gt, ALU.add))

            def place_experts():
                link(dve.tensor_tensor_scan(over[:, 1, :], ones8[:, :], over[:, 0, :], 0.0, ALU.mult, ALU.add))
                link(dve.tensor_tensor(over[:, 2, :], over[:, 1, :], over[:, 0, :], ALU.subtract))
                link(dve.tensor_scalar(base[:, 0, :], over[:, 2, :], ROUTED - 1.0, float(P), ALU.add, ALU.mult))
                link(dve.tensor_tensor(base[:, 1, :], iota128[:, :], base[:, 0, :], ALU.subtract))

            def place_rows():
                link(dve.tensor_scalar(first[:, :, :], rank[:, :, :], P - 0.5, None, ALU.is_lt))
                link(dve.tensor_tensor(first[:, :, :], first[:, :, :],
                                       base[:, 1, :].unsqueeze(1).to_broadcast([P, T, ROUTED]), ALU.mult))
                link(dve.tensor_tensor(row[:, :, :], rank[:, :, :],
                                       base[:, 0, :].unsqueeze(1).to_broadcast([P, T, ROUTED]), ALU.add))
                link(dve.tensor_tensor(row[:, :, :], row[:, :, :], first[:, :, :], ALU.add))

            def place_tokens():
                for k in range(TOP):
                    ins = dve.tensor_tensor(gat[:, k, :, :], hot[:, k, :, :], row[:, :, :], ALU.mult)
                link(ins)
                link(dve.tensor_reduce(rows_of_f[:, :, :], gat[:, :, :, :], AX_X, ALU.add))
                dve.tensor_copy(rows_of[:, :, :], rows_of_f[:, :, :]).then_inc(rows_of_ready, 1)

            def tables():
                link(dve.tensor_tensor(after[:, :, :], over[:, 1, :].unsqueeze(1).to_broadcast([P, OVER, ROUTED]),
                                       over_no[:, :, :], ALU.is_le))
                link(dve.tensor_reduce(expert_f[:, ROUTED:SLOTS], after[:, :, :], AX_X, ALU.add))
                link(dve.tensor_scalar(expert_f[:, ROUTED:SLOTS], expert_f[:, ROUTED:SLOTS], ROUTED - 1.0, None,
                                       ALU.min))
                dve.tensor_copy(expert_of[:, :], expert_f[:, :]).then_inc(expert_ready, 1)

            def gap_of():
                dve.wait_ge(rows_of_ready, 1)
                for k in range(TOP):
                    ins = dve.tensor_tensor(gat[:, k, :, :], hot[:, k, :, :], sg[:, 0, :, :], ALU.mult)
                link(ins)
                link(dve.tensor_reduce(g2[:, :, :], gat[:, :, :, :], AX_X, ALU.add))
                dve.tensor_tensor(gap[:, :], g2[:, 0, :], g2[:, 1, :], ALU.subtract).then_inc(gap_ready, 1)

            def gates():
                dve.wait_ge(tanh_done, 1)
                for k in range(TOP):
                    ins = dve.tensor_scalar(notes[:, k, :, 1], gap[:, :], 0.5 - k, 0.5, ALU.mult, ALU.add)
                ins.then_inc(notes_ready, 1)

            def shared_out(half):
                dve.wait_ge(down_ps, SHARED * J * (half + 1))
                flat = xs[:, 2 * half:2 * half + 2, :].rearrange("p t d -> p (t d)")
                dve.tensor_tensor(flat, bank(SHARED_BANK + half), flat, ALU.add).then_inc(shared_read, 1)

            def rows_copy(n):
                dve.wait_ge(xrowT_ps, n)
                dve.tensor_copy(xrowT[:, :, :].rearrange("p c n -> p (c n)"), bank(SLOT_X_BANK, 0, D)
                                ).then_inc(xrowT_sb, 1)

            def split_down(slot, b, half):
                steps = slice(4 * half, 4 * half + 4)
                dve.wait_ge(dhi_ready, 2 * slot + half + 1)
                dve.tensor_tensor(dlo[b % 2][:, steps, :], ring[b][:, steps, C * P:STEP_W],
                                  dhi[b % 2][:, steps, :].bitcast(F32), ALU.subtract).then_inc(dlo_ready, 1)

            mine = {"T": probT_copy, "x_bias": x_bias, "S": max_chunk, "W": weigh, "mixT": mixT_copy, "proj": x1_stats,
                    "norm2": norm2, "norm3": norm3,
                    "tq": c2_dot, "sc": softmax2, "v": v_copy, "z": x2_add, "xn3T": split_x,
                    "split": lambda q: split_low(q, q % J, q // J % 2),
                    "unit": unit, "lead": stage, "sigmoid": route, "top2": top2,
                    "indices": indices, "hot": mark, "choices": choices, "place": place,
                    "place_experts": place_experts, "place_rows": place_rows, "place_tokens": place_tokens,
                    "tables": tables, "gap": gap_of, "gates": gates, "shared_out": shared_out,
                    "slot_rows": lambda: rows_copy(1), "slot_down": lambda half: split_down(0, 0, half)}
            for what, *args in ORDER:
                if what in mine:
                    mine[what](*args)

            def low_features(slot, half):
                dve.wait_ge(slot_hhi_ready, 2 * slot + half + 1)
                dve.tensor_tensor(slot_hlo[:, half, :], slot_h[:, half, :], slot_hhi[:, half, :].bitcast(F32),
                                  ALU.subtract).then_inc(slot_hlo_ready, 1)

            def slot_step(slot, b, last=False):
                if not last:
                    rows_copy(slot + 2)
                low_features(slot, 1)
                if not last:
                    split_down(slot + 1, (b + 1) % RING, 0)
                    low_features(slot + 1, 0)
                dve.wait_ge(slot_down_ps, slot + 1)
                dve.wait_ge(notes_in, 16)
                dve.tensor_scalar(y_rows[:, bass.ds(slot, 1), :].rearrange("p s d -> p (s d)"),
                                  bank(SLOT_OUT_BANKS[b % 2], 0, D),
                                  slot_notes[:, bass.ds(slot, 1), 1:2].rearrange("p s n -> p (s n)"), None, ALU.mult
                                  ).then_inc(y_rows_ready, 1)
                if not last:
                    split_down(slot + 1, (b + 1) % RING, 1)

            dve.memset(c2[:, :], 0.0).then_inc(y_rows_ready, 2)
            low_features(0, 0)
            with dve.Fori(0, SLOTS // RING) as turn:
                for b in range(RING):
                    slot_step(turn * RING + b, b)
            for b in range(SLOTS % RING):
                slot = SLOTS - SLOTS % RING + b
                slot_step(slot, b, last=slot == SLOTS - 1)
            dve.wait_ge(shared_read, 2)
            for t in range(T):
                dve.wait_ge(picked_in[t], 16)
                for k in range(TOP):
                    ins = dve.tensor_tensor(xs[:, t, :], xs[:, t, :], picked[:, k, t, :], ALU.add)
                    if k < TOP - 1:
                        link(ins)
                ins.then_inc(y_ready, 1)


def kernel(**inputs):
    import numpy as np
    import concourse.bacc as bacc
    from concourse import mybir as mb
    from concourse.bass_utils import run_bass_kernel_spmd

    a = {k: np.asarray(v) for k, v in inputs.items()}

    def up(w):
        return w.reshape(-1, J, P, C, P).transpose(0, 4, 1, 3, 2).reshape(-1, P, J, C * P)

    def down(w):
        return w.reshape(-1, D, J, P).transpose(0, 3, 2, 1)

    squares = np.stack([a["L0_xattn_Wq"].T, a["L0_xattn_Wk"].T, a["L0_xattn_Wv"].T, a["L0_xattn_Wo"],
                        a["L0_attn_Wq"], a["L0_attn_Wk"], a["L0_attn_Wv"].T])
    beside = np.stack([a["L0_xattn_bq"], a["L0_xattn_bk"], a["L0_xattn_bv"], a["L0_xattn_bo"],
                       a["L0_attn_bq"], a["L0_attn_bk"], a["L0_attn_bv"]])
    squares = np.concatenate([squares, beside[:, :, None]], axis=2)
    arrays = {
        "x_in_dram": a["x"].reshape(N, D),
        "ctx_dram": a["ctx_1024"],
        "ctxT_dram": a["ctx_1024"].transpose(0, 2, 1),
        "squares_dram": squares.reshape(7, C, P, D + 1).transpose(2, 0, 1, 3),
        "cols_dram": np.concatenate([np.stack([a["L0_xattn_bq"], a["L0_xattn_bk"], a["L0_xattn_bv"],
                                               a["L0_attn_bq"], a["L0_attn_bk"]]),
                                     a["L0_ffn_centroids"]]).T,
        "rows_dram": np.concatenate([a["L0_xattn_bo"], a["L0_attn_bv"], a["L0_ffn_routing_bias"]]),
        "experts_dram": np.concatenate([
            np.concatenate([up(a["L0_ffn_Wfc_sh"]), down(a["L0_ffn_Wproj_sh"])], axis=3),
            np.concatenate([up(a["L0_ffn_Wfc_r"]), down(a["L0_ffn_Wproj_r"])], axis=3)]),
    }
    arrays = {k: np.ascontiguousarray(v) for k, v in arrays.items()}
    nc = bacc.Bacc("TRN2", target_bir_lowering=False, num_devices=1)
    args = [nc.dram_tensor(k, v.shape, mb.dt.from_np(v.dtype), kind="ExternalInput").ap() for k, v in arrays.items()]
    out = nc.dram_tensor("out_dram", (N, D), mb.dt.float32, kind="ExternalOutput").ap()
    slot_x = nc.dram_tensor("slot_x_dram", (SLOTS * P, D), mb.dt.float32, kind="Internal").ap()
    notes = nc.dram_tensor("notes_dram", (SLOTS * P, 2), mb.dt.float32, kind="Internal").ap()
    results = nc.dram_tensor("results_dram", (TOP * N + SLOTS * P, D), mb.dt.float32, kind="Internal").ap()
    build(nc, *args, out, slot_x, notes, results)
    r = run_bass_kernel_spmd(nc, [arrays], core_ids=[0])
    return r.results[0]["out_dram"].reshape(B, SQ, D)
```
